# Optimizing a Trainium2 kernel written in Bass

```python
import numpy as np
import jax
import jax.numpy as jnp

def _softmax(x, axis=-1):
    return jax.nn.softmax(x, axis=axis)

def _gelu(x):
    return jax.nn.gelu(x, approximate=True)

def _silu(x):
    return jax.nn.silu(x)

def _sigmoid(x):
    return jax.nn.sigmoid(x)

def _layernorm(x, axis=-1, eps=1e-05):
    m = jnp.mean(x, axis=axis, keepdims=True)
    v = jnp.var(x, axis=axis, keepdims=True)
    return (x - m) / jnp.sqrt(v + eps)

def _scatter_add(tgt, idx, src, axis=0):
    return tgt.at[idx].add(src)

def _segment_sum(src, seg, n):
    return jax.ops.segment_sum(src, seg, n)
kernel_name = 'mk_seq_preln_d1_jaxref_r4_a1af7a'

def setup_inputs(seed: int=0):
    np.random.seed(seed)
    _w = jnp.asarray

    def _L0_attn_setup():
        import jax, jax.numpy as jnp
        import numpy as np
        import math
        B, T, E = (1, 512, 256)
        H = 8
        D = E // H // 2
        LAMBDA_INIT = 0.8 - 0.6 * math.exp(-0.3 * 1)
        SCALE_BASE = 512.0
        THETA = 10000.0

        def _rope_tables(T, d):
            inv_freq = 1.0 / THETA ** (jnp.arange(0, d, 2, dtype=jnp.float32) / d)
            pos = jnp.arange(T, dtype=jnp.float32)
            freqs = pos[:, None] * inv_freq[None, :]
            freqs = jnp.repeat(freqs, 2, axis=-1)
            sv = (jnp.arange(0, d, 2, dtype=jnp.float32) + 0.4 * d) / (1.4 * d)
            power = (pos - T // 2) / SCALE_BASE
            scale = sv[None, :] ** power[:, None]
            scale = jnp.concatenate([scale, scale], axis=-1)
            return (freqs, scale)

        def _rotate_half(x):
            x1 = x[..., 0::2]
            x2 = x[..., 1::2]
            return jnp.stack([-x2, x1], axis=-1).reshape(x.shape)

        def _apply_rope(t, freqs, scale):
            f = freqs[None, :, None, :]
            s = scale[None, :, None, :]
            return t * jnp.cos(f) * s + _rotate_half(t) * jnp.sin(f) * s
        key = jax.random.key(seed)
        ks = jax.random.split(key, 9)
        w = 0.02
        return {'x': jax.random.normal(ks[0], (B, T, E), dtype=jnp.float32), 'Wq': jax.random.normal(ks[1], (E, E), dtype=jnp.float32) * w, 'Wk': jax.random.normal(ks[2], (E, E), dtype=jnp.float32) * w, 'Wv': jax.random.normal(ks[3], (E, E), dtype=jnp.float32) * w, 'Wo': jax.random.normal(ks[4], (E, E), dtype=jnp.float32) * w, 'lambda_q1': jax.random.normal(ks[5], (D,), dtype=jnp.float32) * 0.1, 'lambda_k1': jax.random.normal(ks[6], (D,), dtype=jnp.float32) * 0.1, 'lambda_q2': jax.random.normal(ks[7], (D,), dtype=jnp.float32) * 0.1, 'lambda_k2': jax.random.normal(ks[8], (D,), dtype=jnp.float32) * 0.1}
    _L0_attn_in = _L0_attn_setup()

    def _L0_ffn_setup():
        import jax, jax.numpy as jnp
        import numpy as np
        from jax import lax
        T, B, I, M, O = (64, 64, 256, 256, 256)

        def _xavier(key, shape):
            fan_out, fan_in = shape
            limit = float(np.sqrt(6.0 / (fan_in + fan_out)))
            return jax.random.uniform(key, shape, jnp.float32, -limit, limit)
        key = jax.random.key(seed)
        ks = jax.random.split(key, 9)
        x = jax.random.normal(ks[0], (T, B, I), jnp.float32)
        return {'x': x, 'wf': _xavier(ks[1], (M, I)), 'uf': _xavier(ks[2], (M, M)), 'bf': jnp.zeros((M,), jnp.float32), 'wi': _xavier(ks[3], (M, I)), 'ui': _xavier(ks[4], (M, M)), 'bi': jnp.zeros((M,), jnp.float32), 'wc': _xavier(ks[5], (M, I)), 'uc': _xavier(ks[6], (M, M)), 'bc': jnp.zeros((M,), jnp.float32), 'wo': _xavier(ks[7], (O, I)), 'uo': _xavier(ks[8], (O, M)), 'bo': jnp.zeros((O,), jnp.float32), 'in_c': jnp.zeros((M,), jnp.float32)}
    _L0_ffn_in = _L0_ffn_setup()
    _d = {'L0_attn_x': _L0_attn_in['x'], 'L0_attn_Wq': _L0_attn_in['Wq'], 'L0_attn_Wk': _L0_attn_in['Wk'], 'L0_attn_Wv': _L0_attn_in['Wv'], 'L0_attn_Wo': _L0_attn_in['Wo'], 'L0_attn_lambda_q1': _L0_attn_in['lambda_q1'], 'L0_attn_lambda_k1': _L0_attn_in['lambda_k1'], 'L0_attn_lambda_q2': _L0_attn_in['lambda_q2'], 'L0_attn_lambda_k2': _L0_attn_in['lambda_k2'], 'L0_ffn_wf': _L0_ffn_in['wf'], 'L0_ffn_uf': _L0_ffn_in['uf'], 'L0_ffn_bf': _L0_ffn_in['bf'], 'L0_ffn_wi': _L0_ffn_in['wi'], 'L0_ffn_ui': _L0_ffn_in['ui'], 'L0_ffn_bi': _L0_ffn_in['bi'], 'L0_ffn_wc': _L0_ffn_in['wc'], 'L0_ffn_uc': _L0_ffn_in['uc'], 'L0_ffn_bc': _L0_ffn_in['bc'], 'L0_ffn_wo': _L0_ffn_in['wo'], 'L0_ffn_uo': _L0_ffn_in['uo'], 'L0_ffn_bo': _L0_ffn_in['bo'], 'L0_ffn_in_c': _L0_ffn_in['in_c']}
    _x0 = _d['L0_attn_x']
    _d['L0_attn_x'] = jax.random.normal(jax.random.fold_in(jax.random.key(seed), 1), (16, 1024, 256), dtype=_x0.dtype)
    del _x0
    return _d

def reference(L0_attn_x, L0_attn_Wq, L0_attn_Wk, L0_attn_Wv, L0_attn_Wo, L0_attn_lambda_q1, L0_attn_lambda_k1, L0_attn_lambda_q2, L0_attn_lambda_k2, L0_ffn_wf, L0_ffn_uf, L0_ffn_bf, L0_ffn_wi, L0_ffn_ui, L0_ffn_bi, L0_ffn_wc, L0_ffn_uc, L0_ffn_bc, L0_ffn_wo, L0_ffn_uo, L0_ffn_bo, L0_ffn_in_c):

    def _L0_attn_ref(x, Wq, Wk, Wv, Wo, lambda_q1, lambda_k1, lambda_q2, lambda_k2):
        import jax, jax.numpy as jnp
        import numpy as np
        import math
        B, T, E = (1, 512, 256)
        H = 8
        D = E // H // 2
        LAMBDA_INIT = 0.8 - 0.6 * math.exp(-0.3 * 1)
        SCALE_BASE = 512.0
        THETA = 10000.0

        def _rope_tables(T, d):
            inv_freq = 1.0 / THETA ** (jnp.arange(0, d, 2, dtype=jnp.float32) / d)
            pos = jnp.arange(T, dtype=jnp.float32)
            freqs = pos[:, None] * inv_freq[None, :]
            freqs = jnp.repeat(freqs, 2, axis=-1)
            sv = (jnp.arange(0, d, 2, dtype=jnp.float32) + 0.4 * d) / (1.4 * d)
            power = (pos - T // 2) / SCALE_BASE
            scale = sv[None, :] ** power[:, None]
            scale = jnp.concatenate([scale, scale], axis=-1)
            return (freqs, scale)

        def _rotate_half(x):
            x1 = x[..., 0::2]
            x2 = x[..., 1::2]
            return jnp.stack([-x2, x1], axis=-1).reshape(x.shape)

        def _apply_rope(t, freqs, scale):
            f = freqs[None, :, None, :]
            s = scale[None, :, None, :]
            return t * jnp.cos(f) * s + _rotate_half(t) * jnp.sin(f) * s
        b, t, e = x.shape
        scaling = D ** (-0.5)
        q = (x @ Wq.T).reshape(b, t, 2 * H, D)
        k = (x @ Wk.T).reshape(b, t, 2 * H, D)
        v = (x @ Wv.T).reshape(b, t, H, 2 * D)
        freqs, scale = _rope_tables(t, D)
        q = _apply_rope(q, freqs, scale)
        k = _apply_rope(k, freqs, 1.0 / scale)
        q = jnp.transpose(q, (0, 2, 1, 3)) * scaling
        k = jnp.transpose(k, (0, 2, 1, 3))
        v = jnp.transpose(v, (0, 2, 1, 3))
        scores = jnp.einsum('bhtd,bhsd->bhts', q, k)
        probs = jax.nn.softmax(scores.astype(jnp.float32), axis=-1).astype(scores.dtype)
        lam1 = jnp.exp(jnp.sum(lambda_q1 * lambda_k1))
        lam2 = jnp.exp(jnp.sum(lambda_q2 * lambda_k2))
        lam = lam1 - lam2 + LAMBDA_INIT
        probs = probs.reshape(b, H, 2, t, t)
        diff = probs[:, :, 0] - lam * probs[:, :, 1]
        attn = jnp.einsum('bhts,bhsd->bhtd', diff, v)
        attn = attn * jax.lax.rsqrt(jnp.mean(attn * attn, axis=-1, keepdims=True) + 1e-05)
        attn = attn * (1.0 - LAMBDA_INIT)
        attn = jnp.transpose(attn, (0, 2, 1, 3)).reshape(b, t, e)
        return attn @ Wo.T

    def _L0_ffn_ref(x, wf, uf, bf, wi, ui, bi, wc, uc, bc, wo, uo, bo, in_c):
        import jax, jax.numpy as jnp
        import numpy as np
        from jax import lax
        T, B, I, M, O = (64, 64, 256, 256, 256)

        def _xavier(key, shape):
            fan_out, fan_in = shape
            limit = float(np.sqrt(6.0 / (fan_in + fan_out)))
            return jax.random.uniform(key, shape, jnp.float32, -limit, limit)
        batch = x.shape[1]
        c0 = jnp.broadcast_to(in_c, (batch, in_c.shape[0]))

        def step(c, xt):
            ft = jax.nn.sigmoid(xt @ wf.T + c @ uf.T + bf)
            it = jax.nn.sigmoid(xt @ wi.T + c @ ui.T + bi)
            gt = jnp.tanh(xt @ wc.T + c @ uc.T + bc)
            c = ft * c + it * gt
            return (c, None)
        c_final, _ = lax.scan(step, c0, x)
        h = jnp.tanh(jnp.einsum('tbi,oi->tbo', x, wo) + c_final @ uo.T + bo)
        return h
    x = L0_attn_x
    x = x + _L0_attn_ref(_layernorm(x, axis=-1), L0_attn_Wq, L0_attn_Wk, L0_attn_Wv, L0_attn_Wo, L0_attn_lambda_q1, L0_attn_lambda_k1, L0_attn_lambda_q2, L0_attn_lambda_k2)
    x = x + _L0_ffn_ref(_layernorm(x, axis=-1), L0_ffn_wf, L0_ffn_uf, L0_ffn_bf, L0_ffn_wi, L0_ffn_ui, L0_ffn_bi, L0_ffn_wc, L0_ffn_uc, L0_ffn_bc, L0_ffn_wo, L0_ffn_uo, L0_ffn_bo, L0_ffn_in_c)
    return x

_drawn_inputs = setup_inputs


def setup_inputs(seed=0):
    import zlib

    import numpy as np

    out = dict(_drawn_inputs(seed))
    spreads = {'L0_ffn_bf': (0.0, 0.744),
     'L0_ffn_bi': (0.0, 0.701),
     'L0_ffn_bc': (0.0, 0.1),
     'L0_ffn_bo': (0.0, 0.1),
     'L0_ffn_in_c': (0.0, 0.8)}
    factors = {'L0_attn_lambda_q1': 8.0,
     'L0_attn_lambda_k1': 3.929,
     'L0_attn_lambda_q2': 8.0,
     'L0_attn_lambda_k2': 8.0}
    for name, (base, spread) in spreads.items():
        noise = np.random.default_rng([zlib.crc32(name.encode()), seed]).standard_normal(out[name].shape)
        drawn = base * np.exp(spread * noise) if base else spread * noise
        out[name] = jnp.asarray(drawn.astype(out[name].dtype))
    for name, factor in factors.items():
        out[name] = (out[name] * factor).astype(out[name].dtype)
    return out
```

```python
import math
from contextlib import ExitStack

import numpy as np

import concourse.bass as bass
from concourse import mybir

ALU = mybir.AluOpType
ACT = mybir.ActivationFunctionType
AX = mybir.AxisListType
F32 = mybir.dt.float32
BF16 = mybir.dt.bfloat16

P = 128
NB, T, E = 16, 1024, 256
H = 8
D = E // H // 2
TT = T // P
KC = E // P
HALF = T // 2
G = 2
SUBS = 8
BLK = 6
SROWS = BLK * D
KROWS = SROWS + 3
Q_PART = (0, 0, 1, 1, 0, 2)
K_PART = (0, 1, 0, 1, 2, 0)
LAMBDA_INIT = 0.8 - 0.6 * math.exp(-0.3 * 1)
KEEP = 1.0 - LAMBDA_INIT
EPS = 1e-5

XT1, QK0, QK1, VAL, RMS, WO, XT2, GATE, ZED, GEE = 0, 4, 8, 12, 16, 20, 24, 28, 40, 44
PER_ITER = 44
PRE = 16
ACT_ITER = PER_ITER - 4

ROUNDS, KT = 4, 8
STEPS = ROUNDS * KT
LN_STEPS = TT + 7
SCORES = SUBS * TT * 2


def act_index(i):
    return i if i < WO else i - 4


def score_plan(start, per_step):
    plan, at = [], 0
    for s in range(STEPS):
        n = per_step if s >= start else 0
        n = min(n, SCORES - at)
        plan.append(range(at, at + n))
        at += n
    assert at == SCORES
    return plan


PLAN0 = score_plan(2, 5)
PLAN1 = score_plan(9, 6)
NO_PLAN = [range(0)] * STEPS


def build(nc, x, wq, wk, wv, wo_attn, lq1, lk1, lq2, lk2, wf, uf, bf, wi, ui, bi, wc, uc, bc,
          wo, uo, bo, in_c, tables, ident_in, out):
    qk_scr = nc.dram_tensor("qk_parts", (2, 3, P, T), BF16, kind="Internal").ap()
    x2_scr = nc.dram_tensor("x2_rows", (NB, P, TT * E), F32, kind="Internal").ap()
    z_scr = nc.dram_tensor("z_rows", (NB, P, TT * E), F32, kind="Internal").ap()

    with ExitStack() as ctx:
        def sb(name, shape, dt=F32):
            return ctx.enter_context(nc.sbuf_tensor(name, shape, dt))

        def sem(name):
            return ctx.enter_context(nc.semaphore(name))

        q_stack = [sb(f"q_stack{g}", [P, SUBS, T], BF16) for g in range(G)]
        k_stack = [sb(f"k_stack{g}", [P, SUBS, T], BF16) for g in range(G)]
        weights = sb("weights", [P, 11, KC, E])
        W_Q, W_K, W_V, W_O, W_F, W_I, W_C, U_F, U_I, U_C, W_Z = range(11)
        U_Z = W_Q
        rope_tab = sb("rope_tab", [P, 4, T])
        values = sb("values", [P, TT, E])
        probs = [sb(f"probs{i}", [P, 4, HALF]) for i in range(4)]
        pair_sum = sb("pair_sum", [P, 4, HALF])
        xa = sb("xa", [P, TT * E])
        xt = sb("xt", [P, KC, T])
        swapped = sb("swapped", [P, 2, T])
        parts = sb("parts", [P, 3, T], BF16)
        attn_t = sb("attn_t", [P, G, T])
        o_copy = sb("o_copy", [P, 2, HALF])
        inv_sum = sb("inv_sum", [P, HALF])
        cell_t = sb("cell_t", [P, KC, T])
        ident = sb("ident", [P, P])
        head_ones = sb("head_ones", [P, P])
        ones = sb("ones", [P, P])
        gate_bias = sb("gate_bias", [P, 3, KC])
        cell0 = sb("cell0", [P, KC])
        bo_row = sb("bo_row", [1, E])
        lam_in = sb("lam_in", [P, 4, D])
        lam_prod = sb("lam_prod", [P, 2, D])
        lam_dot = sb("lam_dot", [P, 2])
        lam_exp = sb("lam_exp", [P, 2])
        neg_lam = sb("neg_lam", [P, 1])
        rms_eps = sb("rms_eps", [P, 1])
        neg_half = sb("neg_half", [P, TT])
        stats = sb("stats", [P, TT, 6])
        ln_sum, ln_diff, ln_square, ln_between, mean = (
            sb(n, [P, TT]) for n in ("ln_sum", "ln_diff", "ln_square", "ln_between", "mean"))
        var_eps = sb("var_eps", [P, TT])
        rstd = sb("rstd", [P, TT])
        neg_max2 = sb("neg_max2", [P, SUBS * TT, 2])
        neg_max = sb("neg_max", [P, P])
        shift_rest = sb("shift_rest", [SUBS * TT, P])
        shift = sb("shift", [SUBS * TT, 3, P], BF16)

        raw = [xa[:, 0:T], xa[:, T:2 * T]]
        x2 = probs[0][:, :, :].rearrange("p a b -> p (a b)")
        xn2 = probs[1][:, :, :].rearrange("p a b -> p (a b)")
        zed = xn2
        rms = probs[1]
        square = probs[2]
        gates = [probs[2], probs[3]]

        st = [ctx.enter_context(nc.psum_tensor(f"st{i}", [P, 2, HALF], F32)) for i in range(2)]
        s_ps = [ctx.enter_context(nc.psum_tensor(f"s_ps{i}", [P, HALF], F32)) for i in range(2)]
        o_ps = ctx.enter_context(nc.psum_tensor("o_ps", [P, HALF], F32))
        sum_ps = ctx.enter_context(nc.psum_tensor("sum_ps", [P, HALF], F32))

        def ring(i):
            return st[(i % 4) // 2][:, i % 2, :]

        consts_in = sem("consts_in")
        uo_in = sem("uo_in")
        consts_made = sem("consts_made")
        lam_step = sem("lam_step")
        x_in = sem("x_in")
        xr_in = sem("xr_in")
        ln_stat = sem("ln_stat")
        ln_pow = sem("ln_pow")
        ln_out = sem("ln_out")
        ring_ready = sem("ring_ready")
        act_out = sem("act_out")
        wo_added = sem("wo_added")
        swap_in = [sem("swap_q"), sem("swap_k")]
        rope_step = sem("rope_step")
        rope_done = sem("rope_done")
        parts_out = sem("parts_out")
        stack_in = [sem("stack_q"), sem("stack_k")]
        score_ready = sem("score_ready")
        max_done = sem("max_done")
        max_all = sem("max_all")
        max_turned = sem("max_turned")
        shift_step = sem("shift_step")
        shift_made = sem("shift_made")
        shift_in = sem("shift_in")
        st_ready = sem("st_ready")
        exp_done = sem("exp_done")
        pair_added = sem("pair_added")
        av_done = sem("av_done")
        sum_done = sem("sum_done")
        o_read = sem("o_read")
        o_scaled = sem("o_scaled")
        at_ready = sem("at_ready")
        sq_ready = sem("sq_ready")
        rms_inv = sem("rms_inv")
        at_norm = sem("at_norm")
        sum_read = sem("sum_read")
        sum_inv = sem("sum_inv")
        cell_step = sem("cell_step")
        cell_ready = sem("cell_ready")
        x2_out = sem("x2_out")
        z_out = sem("z_out")
        tail_in = [sem(f"tail_in{s}") for s in range(4)]
        tail_add = sem("tail_add")
        tail_tanh = sem("tail_tanh")
        tail_sum = sem("tail_sum")
        tail_out = [sem(f"tail_out{s}") for s in range(4)]

        block = ctx.enter_context(nc.Block())

        def ring_base(b, last):
            return b * PER_ITER + (PRE - (PRE if last else 0))

        def act_base(b, last):
            return b * ACT_ITER + (PRE - (PRE if last else 0))

        tail_x = [q_stack[s // 2][:, 4 * (s % 2):4 * (s % 2) + 4, :].bitcast(F32)
                  .rearrange("p a b -> p (a b)") for s in range(4)]
        tail_z = [k_stack[s // 2][:, 4 * (s % 2):4 * (s % 2) + 4, :].bitcast(F32)
                  .rearrange("p a b -> p (a b)") for s in range(4)]

        N_CONST = 16 * 25

        @block.sync
        def _(sp):
            def value(v):
                return v if isinstance(v, int) else sp.lower_val(v)

            def load_x(b):
                if not (isinstance(b, int) and b == 0):
                    sp.wait_ge(rope_done, 4 * b)
                sp.dma_start(xa[:, :], x[b, :, :]).then_inc(x_in, 16)

            def stack(b, g, ab):
                u = 2 * b + g
                first = isinstance(u, int) and u == 0
                free = isinstance(u, int) and u < 2
                raw_out = [value(ab + (QK1 if g else QK0) + 2 * X + 2) for X in range(2)]
                before = [value(2 * u - 1 + X) for X in range(2)]
                split = [value(2 * u + X + 1) for X in range(2)]
                stacked = value(16 * BLK * u)
                attended = value(64 * (u - 1))
                stored = [value(16 * (2 * u + X + 1)) for X in range(2)]
                for X in range(2):
                    sp.wait_ge(act_out, raw_out[X])
                    if not first:
                        sp.wait_ge(rope_done, before[X])
                    for a in range(2):
                        sp.dma_start(swapped[a:P:2, X, :], raw[X][1 - a:P:2, :])\
                          .then_inc(swap_in[X], 16)
                for X in range(2):
                    sp.wait_ge(rope_done, split[X])
                    if not first:
                        sp.wait_ge(stack_in[X], stacked)
                    sp.dma_start(qk_scr[X, :, :, :].rearrange("a p t -> p a t"), parts[:, :, :])\
                      .then_inc(parts_out, 16)
                if not free:
                    sp.wait_ge(st_ready, attended)
                for X in range(2):
                    sp.wait_ge(parts_out, stored[X])
                    for i in range(BLK):
                        dst = (q_stack, k_stack)[X][g]
                        part = (Q_PART, K_PART)[X][i]
                        sp.dma_start(dst[D * i:D * i + D, :, :],
                                     qk_scr[X, part, :, :].rearrange("(j d) t -> d j t", d=D))\
                          .then_inc(stack_in[X], 16)

            def shift_rows(u, g):
                sp.wait_ge(shift_made, u + 1)
                for i in range(3):
                    sp.dma_start(q_stack[g][SROWS + i:SROWS + i + 1, :, :], shift[:, i, :])\
                      .then_inc(shift_in, 16)

            def iteration(b, last):
                ab = act_base(b, last)
                if not last:
                    load_x(b + 1)
                shift_rows(2 * b + 1, 1)
                if not last:
                    stack(b + 1, 0, ab)
                    shift_rows(2 * b + 2, 0)
                sp.wait_ge(sum_done, 32 * b + 32)
                sp.dma_start(x2, x[b, :, :]).then_inc(xr_in, 16)
                if not last:
                    stack(b + 1, 1, ab)
                sp.wait_ge(wo_added, 4 * b + 4)
                sp.dma_start(x2_scr[b, :, :], x2).then_inc(x2_out, 16)
                sp.wait_ge(act_out, ab + act_index(ZED) + 4)
                sp.dma_start(z_scr[b, :, :], zed).then_inc(z_out, 16)

            load_x(0)
            n = 0
            for a, w in enumerate((wq, wk, wv, wo_attn, wf, wi, wc, uf, ui, uc, wo)):
                sp.dma_start(weights[:, a, :, :], w.rearrange("(c p) n -> p c n", p=P))\
                  .then_inc(consts_in, 16)
                n += 1
            for a in range(4):
                sp.dma_start(rope_tab[:, a, :], tables[a, :, :]).then_inc(consts_in, 16)
                sp.dma_start(lam_in[:, a, :], (lq1, lk1, lq2, lk2)[a]
                             .rearrange("(a n) -> a n", a=1).partition_broadcast(P))\
                  .then_inc(consts_in, 16)
                n += 2
            for a, v in enumerate((bf, bi, bc)):
                sp.dma_start(gate_bias[:, a, :], v)\
                  .then_inc(consts_in, 16)
                n += 1
            sp.dma_start(cell0[:, :], in_c).then_inc(consts_in, 16)
            sp.dma_start(bo_row[:, :], bo.rearrange("(a n) -> a n", a=1)).then_inc(consts_in, 16)
            sp.dma_start(ident[:, :], ident_in).then_inc(consts_in, 16)
            n += 3
            assert N_CONST == 16 * n
            stack(0, 0, 0)
            stack(0, 1, 0)
            shift_rows(0, 0)
            with sp.Fori(0, NB - 1) as b:
                iteration(b, False)
            sp.dma_start(weights[:, U_Z, :, :], uo.rearrange("(c p) n -> p c n", p=P))\
              .then_inc(uo_in, 16)
            iteration(NB - 1, True)
            sp.wait_ge(x2_out, 16 * NB)
            sp.wait_ge(z_out, 16 * NB)
            for s in range(4):
                sp.dma_start(tail_z[s], z_scr[s, :, :]).then_inc(tail_in[s], 16)
                sp.dma_start(tail_x[s], x2_scr[s, :, :]).then_inc(tail_in[s], 16)
            with sp.Fori(1, NB // 4) as it:
                for s in range(4):
                    sp.wait_ge(tail_out[s], 16 * it)
                    sp.dma_start(tail_z[s], z_scr[4 * it + s, :, :]).then_inc(tail_in[s], 16)
                    sp.dma_start(tail_x[s], x2_scr[4 * it + s, :, :]).then_inc(tail_in[s], 16)
            for s in range(4):
                sp.wait_ge(tail_out[s], 16 * (NB // 4))

        @block.gpsimd
        def _(pool):
            pool.memset(ones[:, :], 1.0).then_inc(consts_made, 1)
            pool.memset(neg_half[:, :], -0.5).then_inc(consts_made, 1)
            pool.memset(rms_eps[:, :], EPS * KEEP ** -2).then_inc(consts_made, 1)

            def pair(u, g, q):
                pool.wait_ge(exp_done, 64 * u + 4 * q + 4)
                if g == 1 or q > 0:
                    pool.wait_ge(sum_done, 16 * u + q)
                a = 2 * q
                pool.tensor_tensor(pair_sum[:, :, :], probs[a % 4][:, :, :],
                                   probs[(a + 1) % 4][:, :, :], ALU.add).then_inc(pair_added, 1)

            def inv_sqrt(n):
                pool.wait_ge(ln_stat, LN_STEPS * (n + 1))
                pool.tensor_tensor(rstd[:, :], var_eps[:, :], neg_half[:, :], ALU.pow)\
                    .then_inc(ln_pow, 1)

            def iteration(b, last):
                for g in range(G):
                    for q in range(4 * ROUNDS):
                        pair(2 * b + g, g, q)
                        if g == 0 and q == 6 and not last:
                            inv_sqrt(2 * b + 1)
                inv_sqrt(2 * b + 2 - (1 if last else 0))

            pool.wait_ge(consts_made, 7)
            inv_sqrt(0)
            with pool.Fori(0, NB - 1) as b:
                iteration(b, False)
            iteration(NB - 1, True)
            with pool.Fori(0, NB // 4) as it:
                for s in range(4):
                    pool.wait_ge(tail_tanh, 4 * it + s + 1)
                    pool.tensor_tensor(tail_x[s], tail_x[s], tail_z[s], ALU.add)\
                        .then_inc(tail_sum, 1)
                    pool.wait_ge(tail_sum, 4 * it + s + 1)
                    pool.dma_start(out[4 * it + s, :, :], tail_x[s]).then_inc(tail_out[s], 16)

        @block.scalar
        def _(act):
            act.wait_ge(consts_made, 7)
            act.wait_ge(lam_step, 4)
            act.activation(lam_exp[:, :], lam_dot[:, :], ACT.Exp).then_inc(lam_step, 1)

            def take(rb, i, dst, func=ACT.Copy, **kw):
                act.wait_ge(ring_ready, rb + i + 1)
                act.activation(dst, ring(i), func, **kw).then_inc(act_out, 1)

            def take_xt(rb, first):
                for h in range(2):
                    for c in range(KC):
                        take(rb, first + 2 * h + c, xt[:, c, h * HALF:(h + 1) * HALF])

            def take_qk(rb, u, g):
                for X in range(2):
                    if g == 1:
                        act.wait_ge(rope_done, 2 * u - 1 + X)
                    for h in range(2):
                        take(rb, (QK1 if g else QK0) + 2 * X + h,
                             raw[X][:, h * HALF:(h + 1) * HALF])

            def take_v(rb):
                for j in range(4):
                    take(rb, VAL + j, values[:, 2 * j:2 * j + 2, :].rearrange("p a b -> p (a b)"))

            def copy_o(u, g, r):
                if g == 1 or r > 1:
                    act.wait_ge(at_ready, 2 * u + r // 2)
                act.wait_ge(av_done, 32 * u + 8 * (r + 1))
                act.activation(o_copy[:, r % 2, :], o_ps[:, :], ACT.Copy).then_inc(o_read, 1)

            def copy_sums(u, g, r):
                if g == 1 or r > 0:
                    act.wait_ge(o_scaled, 4 * u + r)
                act.wait_ge(sum_done, 16 * u + 4 * (r + 1))
                act.activation(inv_sum[:, :], sum_ps[:, :], ACT.Copy).then_inc(sum_read, 1)

            def exps(u, g):
                for kk in range(STEPS):
                    if g == 1 or kk >= 4:
                        act.wait_ge(av_done, 32 * u + (kk - 3))
                        act.wait_ge(pair_added, 16 * u + (kk // 2 - 1))
                    for hp in range(2):
                        act.wait_ge(st_ready, 64 * u + (2 * kk + hp + 1))
                        act.activation(probs[kk % 4][:, 2 * hp:2 * hp + 2, :], st[hp][:, :, :],
                                       ACT.Exp).then_inc(exp_done, 1)
                    if kk % 8 == 0 and kk:
                        copy_o(u, g, kk // 8 - 1)
                    if kk % 8 == 3 and kk > 8:
                        copy_sums(u, g, kk // 8 - 1)
                copy_o(u, g, 3)

            def iteration(b, last):
                rb, ab = ring_base(b, last), act_base(b, last)
                exps(2 * b, 0)
                if not last:
                    take_xt(rb, XT1)
                    take_qk(rb, 2 * b + 2, 0)
                copy_sums(2 * b, 0, 3)
                exps(2 * b + 1, 1)
                if not last:
                    take_qk(rb, 2 * b + 3, 1)
                copy_sums(2 * b + 1, 1, 3)
                if not last:
                    take_v(rb)
                for i in range(4):
                    take(rb, RMS + i, rms[:, i, :], ACT.Ln, scale=KEEP ** -2 / (2 * D),
                         bias=rms_eps[:, 0:1])
                for i in range(4):
                    act.wait_ge(act_out, ab + (RMS + i + 1))
                    act.activation(rms[:, i, :], rms[:, i, :], ACT.Exp, scale=-0.5)\
                       .then_inc(rms_inv, 1)
                take_xt(rb, XT2)
                for h in range(2):
                    for m in range(KC):
                        if h == 1:
                            act.wait_ge(cell_ready, 4 * b + (2 + m))
                        for a, func in enumerate((ACT.Sigmoid, ACT.Sigmoid, ACT.Tanh)):
                            take(rb, GATE + 6 * h + 3 * m + a, gates[m][:, a, :], func,
                                 bias=gate_bias[:, a, m:m + 1])
                for j in range(4):
                    take(rb, ZED + j, zed[:, 2 * j * E:2 * (j + 1) * E])
                act.wait_ge(x2_out, 16 * b + 16)
                act.wait_ge(z_out, 16 * b + 16)
                act.wait_ge(cell_ready, 4 * b + 5)

            act.wait_ge(consts_in, N_CONST)
            take_xt(0, XT1)
            take_qk(0, 0, 0)
            take_qk(0, 1, 1)
            take_v(0)
            with act.Fori(0, NB - 1) as b:
                iteration(b, False)
            iteration(NB - 1, True)
            rb = ring_base(NB - 1, True)
            act.wait_ge(x2_out, 16 * NB)
            for j in range(4):
                take(rb, GEE + j, x2[:, 2 * j * E:2 * (j + 1) * E])
            with act.Fori(0, NB // 4) as it:
                for s in range(4):
                    act.wait_ge(tail_add, 4 * it + s + 1)
                    act.activation(tail_z[s], tail_z[s], ACT.Tanh).then_inc(tail_tanh, 1)

        @block.tensor
        def _(pe):
            def turn(i, b, ab):
                p = i - 4
                if WO <= p < WO + 4:
                    pe.wait_ge(wo_added, 4 * b + (p - WO + 1))
                elif not (isinstance(ab, int) and ab + p + 1 <= 0):
                    pe.wait_ge(act_out, ab + (act_index(p) + 1))

            def transposes(first, src, n, b, ab):
                for h in range(2):
                    pe.wait_ge(ln_out, TT * n + (4 * h + 4))
                    for c in range(KC):
                        i = first + 2 * h + c
                        turn(i, b, ab)
                        for t in range(4):
                            at = (4 * h + t) * E + c * P
                            mm = pe.transpose(ring(i)[:, t * P:(t + 1) * P], src[:, at:at + P],
                                              ident[:, :])
                        mm.then_inc(ring_ready, 1)

            def qk(g, b, ab):
                pe.wait_ge(act_out, ab + XT1 + 4)
                for X in range(2):
                    for h in range(2):
                        i = (QK1 if g else QK0) + 2 * X + h
                        turn(i, b, ab)
                        for c in range(KC):
                            mm = pe.matmul(ring(i), weights[:, W_Q + X, c, g * P:(g + 1) * P],
                                           xt[:, c, h * HALF:(h + 1) * HALF],
                                           start=(c == 0), stop=(c == KC - 1))
                        mm.then_inc(ring_ready, 1)

            def rows_out(first, w, src, b, ab, bias=False):
                for j in range(4):
                    i = first + j
                    turn(i, b, ab)
                    for t in range(2):
                        dst = ring(i)[:, t * E:(t + 1) * E]
                        at = (2 * j + t) * P
                        for c in range(KC):
                            mm = pe.matmul(dst, src[:, c, at:at + P], weights[:, w, c, :],
                                           start=(c == 0), stop=(c == KC - 1 and not bias))
                        if bias:
                            mm = pe.matmul(dst, ones[0:1, :], bo_row[:, :], start=False,
                                           stop=True)
                    mm.then_inc(ring_ready, 1)

            def score(u, g, i):
                s, t, h = i // 16, i % 16 // 2, i % 2
                if i >= 2:
                    pe.wait_ge(max_done, SCORES * u + (i - 1))
                pe.matmul(s_ps[i % 2][:, :], q_stack[g][0:SROWS, s, t * P:(t + 1) * P],
                          k_stack[g][0:SROWS, s, h * HALF:(h + 1) * HALF],
                          start=True, stop=True).then_inc(score_ready, 1)

            def score_start(u):
                pe.wait_ge(stack_in[0], 16 * BLK * (u + 1))
                pe.wait_ge(stack_in[1], 16 * BLK * (u + 1))
                if not (isinstance(u, int) and u == 0):
                    pe.wait_ge(shift_made, u)

            def turn_max(u):
                pe.wait_ge(max_all, u + 1)
                pe.transpose(s_ps[0][:, 0:P], neg_max[:, :], ident[:, :])\
                    .then_inc(max_turned, 1)

            def key_tile(u, g, kk, hp):
                th, sub, kt = kk // 16, kk // 8 % 2, kk % 8
                if kk >= 1:
                    pe.wait_ge(exp_done, 64 * u + (2 * kk + hp - 1))
                for j in range(2):
                    s = 2 * (2 * hp + j) + sub
                    mm = pe.matmul(st[hp][:, j, :],
                                   k_stack[g][0:KROWS, s, kt * P:(kt + 1) * P],
                                   q_stack[g][0:KROWS, s, th * HALF:(th + 1) * HALF],
                                   start=True, stop=True)
                mm.then_inc(st_ready, 1)

            def weighted(u, g, kk):
                r, kt = kk // 8, kk % 8
                pe.wait_ge(exp_done, 64 * u + (2 * kk + 2))
                if kt == 0 and (g == 1 or r > 0):
                    pe.wait_ge(o_read, 4 * u + r)
                for h in range(4):
                    at = (4 * g + h) * 2 * D
                    mm = pe.matmul(o_ps[32 * h:32 * h + 32, :], values[:, kt, at:at + 2 * D],
                                   probs[kk % 4][:, h, :], start=(kt == 0), stop=(kt == KT - 1))
                mm.then_inc(av_done, 1)

            def key_sums(u, g, q):
                r, p = q // 4, q % 4
                pe.wait_ge(pair_added, 16 * u + (q + 1))
                if p == 0 and (g == 1 or r > 0):
                    pe.wait_ge(sum_read, 4 * u + r)
                for h in range(4):
                    mm = pe.matmul(sum_ps[32 * h:32 * h + 32, :], ones[:, 0:32],
                                   pair_sum[:, h, :], start=(p == 0), stop=(p == 3))
                mm.then_inc(sum_done, 1)

            def attention(u, g, un, plan):
                pe.wait_ge(shift_in, 48 * (u + 1))
                for s in range(STEPS):
                    todo = list(plan[s])
                    key_tile(u, g, s, 0)
                    if todo and todo[0] == 0:
                        score_start(un)
                    for i in todo[0:1]:
                        score(un, 1 - g, i)
                    key_tile(u, g, s, 1)
                    for i in todo[1:2]:
                        score(un, 1 - g, i)
                    if s >= 1:
                        weighted(u, g, s - 1)
                    for i in todo[2:4]:
                        score(un, 1 - g, i)
                    if s >= 4 and s % 2 == 0:
                        key_sums(u, g, (s - 4) // 2)
                    for i in todo[4:]:
                        score(un, 1 - g, i)
                weighted(u, g, STEPS - 1)

            def last_sums(u, g):
                key_sums(u, g, 14)
                key_sums(u, g, 15)

            def iteration(b, last):
                ab = act_base(b, last)
                pe.wait_ge(act_out, b * ACT_ITER + PRE)
                attention(2 * b, 0, 2 * b + 1, PLAN0)
                turn_max(2 * b + 1)
                if not last:
                    transposes(XT1, xa, 2 * b + 1, b, ab)
                    qk(0, b, ab)
                last_sums(2 * b, 0)
                if not last:
                    pe.wait_ge(act_out, ab + QK0 + 4)
                attention(2 * b + 1, 1, 2 * b + 2, NO_PLAN if last else PLAN1)
                if not last:
                    turn_max(2 * b + 2)
                    qk(1, b, ab)
                last_sums(2 * b + 1, 1)
                if not last:
                    rows_out(VAL, W_V, xt, b, ab)
                for i in range(4):
                    pe.wait_ge(sq_ready, 4 * b + (i + 1))
                    turn(RMS + i, b, ab)
                    pe.matmul(ring(RMS + i), head_ones[:, :], square[:, i, :], start=True,
                              stop=True).then_inc(ring_ready, 1)
                pe.wait_ge(at_norm, 4 * b + 4)
                rows_out(WO, W_O, attn_t, b, ab)
                transposes(XT2, xn2, 2 * b + 2 - (1 if last else 0), b, ab)
                pe.wait_ge(act_out, ab + act_index(XT2) + 4)
                pe.wait_ge(cell_ready, 4 * b + 1)
                for h in range(2):
                    hs = slice(h * HALF, (h + 1) * HALF)
                    for m in range(KC):
                        ms = slice(m * P, (m + 1) * P)
                        for a in range(3):
                            i = GATE + 6 * h + 3 * m + a
                            turn(i, b, ab)
                            for c in range(KC):
                                pe.matmul(ring(i), weights[:, W_F + a, c, ms], xt[:, c, hs],
                                          start=(c == 0), stop=False)
                            for c in range(KC):
                                mm = pe.matmul(ring(i), weights[:, U_F + a, c, ms],
                                               cell_t[:, c, hs], start=False,
                                               stop=(c == KC - 1))
                            mm.then_inc(ring_ready, 1)
                rows_out(ZED, W_Z, xt, b, ab)

            pe.wait_ge(consts_in, N_CONST)
            pe.wait_ge(consts_made, 7)
            transposes(XT1, xa, 0, 0, 0)
            qk(0, 0, 0)
            qk(1, 0, 0)
            rows_out(VAL, W_V, xt, 0, 0)
            score_start(0)
            for i in range(SCORES):
                score(0, 0, i)
            turn_max(0)
            with pe.Fori(0, NB - 1) as b:
                iteration(b, False)
            iteration(NB - 1, True)
            pe.wait_ge(cell_ready, 4 * NB + 1)
            pe.wait_ge(uo_in, 16)
            rows_out(GEE, U_Z, cell_t, NB - 1, act_base(NB - 1, True), bias=True)

        @block.vector
        def _(dve):
            def norm_stats(n, src):
                for t in range(TT):
                    dve.bn_stats(stats[:, t, :], src[:, t * E:(t + 1) * E]).then_inc(ln_stat, 1)
                even, odd = stats[:, :, 0:3], stats[:, :, 3:6]
                dve.wait_ge(ln_stat, LN_STEPS * n + TT)
                dve.tensor_tensor(ln_sum[:, :], even[:, :, 1], odd[:, :, 1], ALU.add)\
                   .then_inc(ln_stat, 1)
                dve.tensor_tensor(ln_diff[:, :], even[:, :, 1], odd[:, :, 1], ALU.subtract)\
                   .then_inc(ln_stat, 1)
                dve.tensor_tensor(ln_square[:, :], even[:, :, 2], odd[:, :, 2], ALU.add)\
                   .then_inc(ln_stat, 1)
                dve.wait_ge(ln_stat, LN_STEPS * n + TT + 3)
                dve.tensor_scalar(mean[:, :], ln_sum[:, :], 0.5, None, ALU.mult)\
                   .then_inc(ln_stat, 1)
                dve.scalar_tensor_tensor(out=ln_between[:, :], in0=ln_diff[:, :], scalar=0.25,
                                         in1=ln_diff[:, :], op0=ALU.mult, op1=ALU.mult)\
                   .then_inc(ln_stat, 1)
                dve.tensor_scalar(ln_square[:, :], ln_square[:, :], 1.0 / E, EPS, ALU.mult,
                                  ALU.add).then_inc(ln_stat, 1)
                dve.wait_ge(ln_stat, LN_STEPS * n + TT + 6)
                dve.tensor_tensor(var_eps[:, :], ln_square[:, :], ln_between[:, :], ALU.add)\
                   .then_inc(ln_stat, 1)

            def normalise(n, src, dst):
                dve.wait_ge(ln_pow, n + 1)
                for t in range(TT):
                    dve.tensor_scalar(dst[:, t * E:(t + 1) * E], src[:, t * E:(t + 1) * E],
                                      mean[:, t:t + 1], rstd[:, t:t + 1], ALU.subtract,
                                      ALU.mult).then_inc(ln_out, 1)

            def rope(u):
                for X in range(2):
                    n = 2 * u + X
                    first = isinstance(n, int) and n == 0
                    dve.wait_ge(swap_in[X], 32 * (u + 1))
                    dve.tensor_tensor(raw[X], raw[X], rope_tab[:, 2 * X, :], ALU.mult)\
                       .then_inc(rope_step, 1)
                    dve.tensor_tensor(swapped[:, X, :], swapped[:, X, :],
                                      rope_tab[:, 2 * X + 1, :], ALU.mult).then_inc(rope_step, 1)
                    dve.wait_ge(rope_step, 6 * n + 2)
                    dve.tensor_tensor(raw[X], raw[X], swapped[:, X, :], ALU.add)\
                       .then_inc(rope_step, 1)
                    dve.wait_ge(rope_step, 6 * n + 3)
                    if not first:
                        dve.wait_ge(parts_out, 16 * n)
                    dve.tensor_copy(parts[:, 0, :], raw[X]).then_inc(rope_step, 1)
                    dve.wait_ge(rope_step, 6 * n + 4)
                    dve.tensor_tensor(swapped[:, X, :], raw[X], parts[:, 0, :], ALU.subtract)\
                       .then_inc(rope_step, 1)
                    dve.wait_ge(rope_step, 6 * n + 5)
                    dve.tensor_copy(parts[:, 1, :], swapped[:, X, :]).then_inc(rope_step, 1)
                    dve.wait_ge(rope_step, 6 * n + 6)
                    dve.tensor_tensor(parts[:, 2, :], swapped[:, X, :], parts[:, 1, :],
                                      ALU.subtract).then_inc(rope_done, 1)

            def maximum(u, i):
                dve.wait_ge(score_ready, SCORES * u + (i + 1))
                dve.tensor_reduce(neg_max2[:, i // 2, i % 2:i % 2 + 1], s_ps[i % 2][:, :], AX.X,
                                  ALU.max, negate=True).then_inc(max_done, 1)

            def join_max(u):
                dve.wait_ge(max_done, SCORES * (u + 1))
                dve.tensor_reduce(neg_max[:, 0:SUBS * TT], neg_max2[:, :, :], AX.X, ALU.min)\
                   .then_inc(max_all, 1)

            def split_shift(u):
                src = s_ps[0][0:SUBS * TT, 0:P]
                dve.wait_ge(max_turned, u + 1)
                if not (isinstance(u, int) and u == 0):
                    dve.wait_ge(shift_in, 48 * u)
                dve.tensor_copy(shift[:, 0, :], src).then_inc(shift_step, 1)
                dve.wait_ge(shift_step, 3 * u + 1)
                dve.tensor_tensor(shift_rest[:, :], src, shift[:, 0, :], ALU.subtract)\
                   .then_inc(shift_step, 1)
                dve.wait_ge(shift_step, 3 * u + 2)
                dve.tensor_copy(shift[:, 1, :], shift_rest[:, :]).then_inc(shift_step, 1)
                dve.wait_ge(shift_step, 3 * u + 3)
                dve.tensor_tensor(shift[:, 2, :], shift_rest[:, :], shift[:, 1, :],
                                  ALU.subtract).then_inc(shift_made, 1)

            def invert_sums(u, r, part):
                if part == 0:
                    dve.wait_ge(sum_read, 4 * u + (r + 1))
                cols = inv_sum[:, part * P:(part + 1) * P]
                dve.reciprocal(cols, cols).then_inc(sum_inv, 1)

            def divide(u, g, r):
                dve.wait_ge(sum_inv, 16 * u + 4 * (r + 1))
                dve.wait_ge(o_read, 4 * u + (r + 1))
                dve.tensor_tensor(o_copy[:, r % 2, :], o_copy[:, r % 2, :], inv_sum[:, :],
                                  ALU.mult).then_inc(o_scaled, 1)
                if r % 2 == 1:
                    th = r // 2
                    dve.wait_ge(o_scaled, 4 * u + (r + 1))
                    dve.scalar_tensor_tensor(out=attn_t[:, g, th * HALF:(th + 1) * HALF],
                                             in0=o_copy[:, 1, :], scalar=neg_lam[:, 0:1],
                                             in1=o_copy[:, 0, :], op0=ALU.mult, op1=ALU.add)\
                       .then_inc(at_ready, 1)

            def attention(u, g, un, plan, norm=None):
                for s in range(STEPS):
                    for i in plan[s]:
                        maximum(un, i)
                    if norm is not None and s == 9:
                        dve.wait_ge(x_in, 16 * (norm + 1))
                        norm_stats(2 * norm - 1, xa)
                    if norm is not None and s == 20:
                        normalise(2 * norm - 1, xa, xa)
                    if s > 8 and 3 <= s % 8 <= 6:
                        invert_sums(u, s // 8 - 1, s % 8 - 3)
                    if s > 8 and s % 8 == 7:
                        divide(u, g, s // 8 - 1)

            def iteration(b, last):
                rb, ab = ring_base(b, last), act_base(b, last)
                u = 2 * b
                attention(u, 0, u + 1, PLAN0, None if last else b + 1)
                join_max(u + 1)
                split_shift(u + 1)
                for k in range(4):
                    invert_sums(u, 3, k)
                divide(u, 0, 3)
                if not last:
                    rope(u + 2)
                attention(u + 1, 1, u + 2, NO_PLAN if last else PLAN1)
                if not last:
                    join_max(u + 2)
                    split_shift(u + 2)
                for k in range(4):
                    invert_sums(u + 1, 3, k)
                divide(u + 1, 1, 3)
                for i in range(4):
                    g, th = i // 2, i % 2
                    part = attn_t[:, g, th * HALF:(th + 1) * HALF]
                    dve.wait_ge(at_ready, 4 * b + (i + 1))
                    dve.tensor_tensor(square[:, i, :], part, part, ALU.mult).then_inc(sq_ready, 1)
                for i in range(4):
                    g, th = i // 2, i % 2
                    part = attn_t[:, g, th * HALF:(th + 1) * HALF]
                    dve.wait_ge(rms_inv, 4 * b + (i + 1))
                    dve.tensor_tensor(part, part, rms[:, i, :], ALU.mult).then_inc(at_norm, 1)
                dve.wait_ge(xr_in, 16 * (b + 1))
                for j in range(4):
                    rows = x2[:, 2 * j * E:2 * (j + 1) * E]
                    dve.wait_ge(ring_ready, rb + (WO + j + 1))
                    dve.tensor_tensor(rows, ring(WO + j), rows, ALU.add).then_inc(wo_added, 1)
                dve.wait_ge(wo_added, 4 * b + 4)
                n = 2 * b + 2 - (1 if last else 0)
                norm_stats(n, x2)
                normalise(n, x2, xn2)
                if not last:
                    rope(u + 3)
                for h in range(2):
                    dve.wait_ge(act_out, ab + (act_index(GATE) + 6 * h + 6))
                    for m in range(KC):
                        f, i, a = (gates[m][:, j, :] for j in range(3))
                        c = cell_t[:, m, h * HALF:(h + 1) * HALF]
                        dve.tensor_tensor(i, i, a, ALU.mult).then_inc(cell_step, 1)
                        dve.tensor_tensor(f, f, c, ALU.mult).then_inc(cell_step, 1)
                        dve.wait_ge(cell_step, 8 * b + (4 * h + 2 * m + 2))
                        dve.tensor_tensor(c, f, i, ALU.add).then_inc(cell_ready, 1)

            dve.memset(head_ones[:, :], 0.0).then_inc(lam_step, 1)
            dve.wait_ge(lam_step, 1)
            for h in range(4):
                mm = dve.memset(head_ones[32 * h:32 * h + 32, 32 * h:32 * h + 32], 1.0)
            mm.then_inc(consts_made, 1)
            for g in range(G):
                dve.memset(k_stack[g][SROWS:P, :, :], 1.0).then_inc(consts_made, 1)
            dve.wait_ge(x_in, 16)
            norm_stats(0, xa)
            dve.wait_ge(consts_in, N_CONST)
            for a in range(2):
                dve.tensor_tensor(lam_prod[:, a, :], lam_in[:, 2 * a, :], lam_in[:, 2 * a + 1, :],
                                  ALU.mult).then_inc(lam_step, 1)
            dve.wait_ge(lam_step, 3)
            dve.tensor_reduce(lam_dot[:, :], lam_prod[:, :, :], AX.X, ALU.add)\
               .then_inc(lam_step, 1)
            dve.memset(neg_max[:, SUBS * TT:P], 0.0)
            dve.memset(cell_t[:, :, :], 0.0).then_inc(consts_made, 1)
            dve.wait_ge(consts_made, 7)
            for c in range(KC):
                mm = dve.tensor_scalar(cell_t[:, c, :], cell_t[:, c, :], cell0[:, c:c + 1], None,
                                       ALU.add)
            mm.then_inc(cell_ready, 1)
            normalise(0, xa, xa)
            dve.wait_ge(lam_step, 5)
            dve.tensor_tensor(neg_lam[:, :], lam_exp[:, 1:2], lam_exp[:, 0:1], ALU.subtract)\
               .then_inc(lam_step, 1)
            dve.wait_ge(lam_step, 6)
            dve.tensor_scalar(neg_lam[:, :], neg_lam[:, :], -LAMBDA_INIT, None, ALU.add)\
               .then_inc(lam_step, 1)
            rope(0)
            rope(1)
            for i in range(SCORES):
                maximum(0, i)
            join_max(0)
            split_shift(0)
            dve.wait_ge(lam_step, 7)
            with dve.Fori(0, NB - 1) as b:
                iteration(b, False)
            iteration(NB - 1, True)
            dve.wait_ge(act_out, act_base(NB - 1, True) + act_index(GEE) + 4)
            with dve.Fori(0, NB // 4) as it:
                for s in range(4):
                    dve.wait_ge(tail_in[s], 32 * it + 32)
                    dve.tensor_tensor(tail_z[s], tail_z[s], x2, ALU.add).then_inc(tail_add, 1)


def rope_tables():
    f32 = np.float32
    even = np.arange(0, D, 2, dtype=f32)
    inv_freq = f32(1.0) / np.power(f32(10000.0), even / f32(D), dtype=f32)
    pos = np.arange(T, dtype=f32)
    freqs = np.repeat(pos[:, None] * inv_freq[None, :], 2, axis=-1).astype(np.float64)
    sv = (even + f32(0.4 * D)) / f32(1.4 * D)
    power = (pos - T // 2) / f32(512.0)
    scale = np.power(sv[None, :].astype(np.float64), power[:, None].astype(np.float64))
    scale = np.concatenate([scale, scale], axis=-1)
    cos, sin = np.cos(freqs), np.sin(freqs)
    sin[:, 0::2] *= -1.0
    q, k = scale * D ** -0.5, 1.0 / scale
    token = (np.arange(P)[None, :] * TT + np.arange(TT)[:, None]).reshape(-1)
    tabs = [np.tile(a[token].T, (SUBS, 1)) for a in (cos * q, sin * q, cos * k, sin * k)]
    return np.ascontiguousarray(np.stack(tabs).astype(f32))


_NAMES = ["attn_Wq", "attn_Wk", "attn_Wv", "attn_Wo", "attn_lambda_q1", "attn_lambda_k1",
          "attn_lambda_q2", "attn_lambda_k2", "ffn_wf", "ffn_uf", "ffn_bf", "ffn_wi", "ffn_ui",
          "ffn_bi", "ffn_wc", "ffn_uc", "ffn_bc", "ffn_wo", "ffn_uo", "ffn_bo", "ffn_in_c"]


def kernel(**inputs):
    import concourse.bacc as _bacc
    from concourse.bass_utils import run_bass_kernel_spmd as _run

    nc = _bacc.Bacc("TRN2", target_bir_lowering=False, num_devices=1)
    arrays = {"x": np.ascontiguousarray(inputs["L0_attn_x"]).reshape(NB, P, TT * E)}
    for name in _NAMES:
        a = np.asarray(inputs["L0_" + name])
        if name in ("ffn_bf", "ffn_bi", "ffn_bc", "ffn_in_c"):
            a = a.reshape(KC, P)
        arrays[name] = np.ascontiguousarray(a.T)
    arrays["rope_tables"] = rope_tables()
    arrays["identity"] = np.eye(P, dtype=np.float32)
    args = [nc.dram_tensor("in_" + n, a.shape, mybir.dt.from_np(a.dtype),
                           kind="ExternalInput").ap() for n, a in arrays.items()]
    out = nc.dram_tensor("out_rows", (NB, P, TT * E), F32, kind="ExternalOutput").ap()
    build(nc, *args, out)
    r = _run(nc, [{"in_" + n: a for n, a in arrays.items()}], core_ids=[0])
    return r.results[0]["out_rows"].reshape(NB, T, E)
```

```python
import itertools
import math
from contextlib import ExitStack

import numpy as np

import concourse.bass as bass
from concourse import mybir

ALU = mybir.AluOpType
ACT = mybir.ActivationFunctionType
AX = mybir.AxisListType
F32 = mybir.dt.float32
BF16 = mybir.dt.bfloat16

P = 128
NB, T, E = 16, 1024, 256
H = 8
D = E // H // 2
TT = T // P
KC = E // P
HALF = T // 2
G = 2
SUBS = 8
BLK = 6
SROWS = BLK * D
KROWS = SROWS + 3
Q_PART = (0, 0, 1, 1, 0, 2)
K_PART = (0, 1, 0, 1, 2, 0)
LAMBDA_INIT = 0.8 - 0.6 * math.exp(-0.3 * 1)
KEEP = 1.0 - LAMBDA_INIT
EPS = 1e-5

QK0, QK1, VAL, RMS, WO, GATE, ZED, GEE = 0, 4, 8, 12, 16, 20, 32, 36
PER_ITER = 36
PRE = 12
ACT_ITER = PER_ITER - 4

ROUNDS, KT = 4, 8
STEPS = ROUNDS * KT
LN_STEPS = TT + 7
SCORES = SUBS * TT * 2


def act_index(i):
    return i if i < WO else i - 4


LATE = (8, 12)
EARLY = (12, 16, 8)


def score_plan(first, last, start):
    n, steps = last - first, STEPS - start
    cuts = [first + (n * s + steps // 2) // steps for s in range(steps + 1)]
    return [range(0)] * start + [range(a, b) for a, b in zip(cuts, cuts[1:])]


PLAN0 = score_plan(sum(EARLY), SCORES, 0)
PLAN1 = score_plan(0, SCORES - sum(LATE), 2)
NO_PLAN = [range(0)] * STEPS


def build(nc, x, wq, wk, wv, wo_attn, lq1, lk1, lq2, lk2, wf, uf, bf, wi, ui, bi, wc, uc, bc,
          wo, uo, bo, in_c, tables, ident_in, out):
    qk_scr = nc.dram_tensor("qk_parts", (2, 3, P, T), BF16, kind="Internal").ap()
    x2_scr = nc.dram_tensor("x2_rows", (NB, P, TT * E), F32, kind="Internal").ap()
    z_scr = nc.dram_tensor("z_rows", (NB, P, TT * E), F32, kind="Internal").ap()

    with ExitStack() as ctx:
        def sb(name, shape, dt=F32):
            return ctx.enter_context(nc.sbuf_tensor(name, shape, dt))

        def sem(name):
            return ctx.enter_context(nc.semaphore(name))

        q_stack = [sb(f"q_stack{g}", [P, SUBS, T], BF16) for g in range(G)]
        k_stack = [sb(f"k_stack{g}", [P, SUBS, T], BF16) for g in range(G)]
        weights = sb("weights", [P, 11, KC, E])
        W_Q, W_K, W_V, W_O, W_F, W_I, W_C, U_F, U_I, U_C, W_Z = range(11)
        U_Z = W_Q
        rope_tab = sb("rope_tab", [P, 4, T])
        values = sb("values", [P, TT, E])
        probs = [sb(f"probs{i}", [P, 4, HALF]) for i in range(4)]
        pair_sum = sb("pair_sum", [P, 4, HALF])
        xa = sb("xa", [P, TT * E])
        xt = sb("xt", [P, KC, T])
        swapped = sb("swapped", [P, 2, T])
        parts = sb("parts", [P, 3, T], BF16)
        attn_t = sb("attn_t", [P, G, T])
        o_copy = sb("o_copy", [P, 2, HALF])
        inv_sum = sb("inv_sum", [P, HALF])
        cell_t = sb("cell_t", [P, KC, T])
        ident = sb("ident", [P, P])
        head_ones = sb("head_ones", [P, P])
        ones = sb("ones", [P, P])
        gate_bias = sb("gate_bias", [P, 3, KC])
        cell0 = sb("cell0", [P, KC])
        bo_row = sb("bo_row", [1, E])
        lam_in = sb("lam_in", [P, 4, D])
        lam_prod = sb("lam_prod", [P, 2, D])
        lam_dot = sb("lam_dot", [P, 2])
        lam_exp = sb("lam_exp", [P, 2])
        neg_lam = sb("neg_lam", [P, 1])
        rms_eps = sb("rms_eps", [P, 1])
        neg_half = sb("neg_half", [P, TT])
        count_start = sb("count_start", [P, 2])
        stats = sb("stats", [P, TT, 6])
        ln_sum, ln_diff, ln_square, ln_between, mean = (
            sb(n, [P, TT]) for n in ("ln_sum", "ln_diff", "ln_square", "ln_between", "mean"))
        var_eps = sb("var_eps", [P, TT])
        rstd = sb("rstd", [P, TT])
        neg_max2 = sb("neg_max2", [P, SUBS * TT, 2])
        neg_max = sb("neg_max", [P, P])
        shift_rest = sb("shift_rest", [SUBS * TT, P])
        shift = sb("shift", [SUBS * TT, 3, P], BF16)

        raw = [xa[:, 0:T], xa[:, T:2 * T]]
        x2 = probs[0][:, :, :].rearrange("p a b -> p (a b)")
        xn2 = probs[1][:, :, :].rearrange("p a b -> p (a b)")
        zed = xn2
        rms = probs[1]
        square = probs[2]
        gates = [probs[2], probs[3]]

        st = [ctx.enter_context(nc.psum_tensor(f"st{i}", [P, 2, HALF], F32)) for i in range(2)]
        s_ps = [ctx.enter_context(nc.psum_tensor(f"s_ps{i}", [P, HALF], F32)) for i in range(2)]
        o_ps = ctx.enter_context(nc.psum_tensor("o_ps", [P, HALF], F32))
        sum_ps = ctx.enter_context(nc.psum_tensor("sum_ps", [P, HALF], F32))

        xt_ps = [o_ps, sum_ps]

        def ring(i):
            return st[(i % 4) // 2][:, i % 2, :]

        consts_in = sem("consts_in")
        uo_in = sem("uo_in")
        consts_made = sem("consts_made")
        lam_step = sem("lam_step")
        x_in = sem("x_in")
        xr_in = sem("xr_in")
        ln_stat = sem("ln_stat")
        ln_pow = sem("ln_pow")
        ln1_out = sem("ln1_out")
        ln2_out = sem("ln2_out")
        xt_ready = sem("xt_ready")
        xt_out = sem("xt_out")
        ring_ready = sem("ring_ready")
        act_out = sem("act_out")
        wo_added = sem("wo_added")
        swap_in = [sem("swap_q"), sem("swap_k")]
        rope_step = sem("rope_step")
        rope_done = sem("rope_done")
        parts_out = sem("parts_out")
        stack_in = [sem("stack_q"), sem("stack_k")]
        score_ready = sem("score_ready")
        max_done = sem("max_done")
        max_all = sem("max_all")
        max_turned = sem("max_turned")
        shift_step = sem("shift_step")
        shift_made = sem("shift_made")
        shift_in = sem("shift_in")
        st_ready = sem("st_ready")
        exp_done = sem("exp_done")
        pair_added = sem("pair_added")
        av_done = sem("av_done")
        sum_done = sem("sum_done")
        o_read = sem("o_read")
        o_scaled = sem("o_scaled")
        at_ready = sem("at_ready")
        sq_ready = sem("sq_ready")
        rms_inv = sem("rms_inv")
        at_norm = sem("at_norm")
        sum_read = sem("sum_read")
        sum_inv = sem("sum_inv")
        cell_step = sem("cell_step")
        cell_ready = sem("cell_ready")
        x2_out = sem("x2_out")
        z_out = sem("z_out")
        tail_in = [sem(f"tail_in{s}") for s in range(4)]
        tail_add = sem("tail_add")
        tail_tanh = sem("tail_tanh")
        tail_sum = sem("tail_sum")
        tail_out = [sem(f"tail_out{s}") for s in range(4)]

        block = ctx.enter_context(nc.Block())

        def ring_base(b, last):
            return b * PER_ITER + (PRE - (PRE if last else 0))

        def act_base(b, last):
            return b * ACT_ITER + (PRE - (PRE if last else 0))

        tail_x = [q_stack[s // 2][:, 4 * (s % 2):4 * (s % 2) + 4, :].bitcast(F32)
                  .rearrange("p a b -> p (a b)") for s in range(4)]
        tail_z = [k_stack[s // 2][:, 4 * (s % 2):4 * (s % 2) + 4, :].bitcast(F32)
                  .rearrange("p a b -> p (a b)") for s in range(4)]

        N_CONST = 16 * 25

        @block.sync
        def _(sp):
            def value(v):
                return v if isinstance(v, int) else sp.lower_val(v)

            def swap(u, g, ab):
                first = isinstance(u, int) and u == 0
                raw_out = [value(ab + (QK1 if g else QK0) + 2 * X + 2) for X in range(2)]
                before = [value(2 * u - 1 + X) for X in range(2)]
                for X in range(2):
                    sp.wait_ge(act_out, raw_out[X])
                    if not first:
                        sp.wait_ge(rope_done, before[X])
                    for a in range(2):
                        sp.dma_start(swapped[a:P:2, X, :], raw[X][1 - a:P:2, :])\
                          .then_inc(swap_in[X], 16)

            def store_parts(u):
                first = isinstance(u, int) and u == 0
                split = [value(2 * u + X + 1) for X in range(2)]
                stacked = value(16 * BLK * u)
                for X in range(2):
                    sp.wait_ge(rope_done, split[X])
                    if not first:
                        sp.wait_ge(stack_in[X], stacked)
                    sp.dma_start(qk_scr[X, :, :, :].rearrange("a p t -> p a t"), parts[:, :, :])\
                      .then_inc(parts_out, 16)

            def stack(u, g):
                attended = value(64 * (u - 1))
                stored = [value(16 * (2 * u + X + 1)) for X in range(2)]
                if not (isinstance(u, int) and u < 2):
                    sp.wait_ge(st_ready, attended)
                for X in range(2):
                    sp.wait_ge(parts_out, stored[X])
                    for i in range(BLK):
                        dst = (q_stack, k_stack)[X][g]
                        part = (Q_PART, K_PART)[X][i]
                        sp.dma_start(dst[D * i:D * i + D, :, :],
                                     qk_scr[X, part, :, :].rearrange("(j d) t -> d j t", d=D))\
                          .then_inc(stack_in[X], 16)

            def shift_rows(u, g):
                sp.wait_ge(shift_made, u + 1)
                for i in range(3):
                    sp.dma_start(q_stack[g][SROWS + i:SROWS + i + 1, :, :], shift[:, i, :])\
                      .then_inc(shift_in, 16)

            def iteration(b, last):
                ab = act_base(b, last)
                u = 2 * b
                if not last:
                    swap(u + 2, 0, ab)
                    store_parts(u + 2)
                shift_rows(u + 1, 1)
                if not last:
                    stack(u + 2, 0)
                    swap(u + 3, 1, ab)
                    store_parts(u + 3)
                    sp.dma_start(xa[:, :], x[(b + 2) & (NB - 1), :, :]).then_inc(x_in, 16)
                    stack(u + 3, 1)
                sp.wait_ge(sum_done, 32 * b + 32)
                sp.dma_start(x2, x[b, :, :]).then_inc(xr_in, 16)
                if not last:
                    shift_rows(u + 2, 0)
                sp.wait_ge(wo_added, 4 * b + 4)
                sp.dma_start(x2_scr[b, :, :], x2).then_inc(x2_out, 16)
                sp.wait_ge(act_out, ab + act_index(ZED) + 4)
                sp.dma_start(z_scr[b, :, :], zed).then_inc(z_out, 16)

            sp.dma_start(xa[:, :], x[0, :, :]).then_inc(x_in, 16)
            n = 0
            for a, w in enumerate((wq, wk, wv, wo_attn, wf, wi, wc, uf, ui, uc, wo)):
                sp.dma_start(weights[:, a, :, :], w.rearrange("(c p) n -> p c n", p=P))\
                  .then_inc(consts_in, 16)
                n += 1
            for a in range(4):
                sp.dma_start(rope_tab[:, a, :], tables[a, :, :]).then_inc(consts_in, 16)
                sp.dma_start(lam_in[:, a, :], (lq1, lk1, lq2, lk2)[a]
                             .rearrange("(a n) -> a n", a=1).partition_broadcast(P))\
                  .then_inc(consts_in, 16)
                n += 2
            for a, v in enumerate((bf, bi, bc)):
                sp.dma_start(gate_bias[:, a, :], v)\
                  .then_inc(consts_in, 16)
                n += 1
            sp.dma_start(cell0[:, :], in_c).then_inc(consts_in, 16)
            sp.dma_start(bo_row[:, :], bo.rearrange("(a n) -> a n", a=1)).then_inc(consts_in, 16)
            sp.dma_start(ident[:, :], ident_in).then_inc(consts_in, 16)
            n += 3
            assert N_CONST == 16 * n
            for u in range(2):
                swap(u, u, 0)
                store_parts(u)
                stack(u, u)
            sp.wait_ge(rope_done, 4)
            sp.dma_start(xa[:, :], x[1, :, :]).then_inc(x_in, 16)
            shift_rows(0, 0)
            with sp.Fori(0, NB - 1) as b:
                iteration(b, False)
            sp.dma_start(weights[:, U_Z, :, :], uo.rearrange("(c p) n -> p c n", p=P))\
              .then_inc(uo_in, 16)
            iteration(NB - 1, True)
            sp.wait_ge(x2_out, 16 * (NB + 1))
            sp.wait_ge(z_out, 16 * (NB + 1))
            for s in range(4):
                sp.dma_start(tail_z[s], z_scr[s, :, :]).then_inc(tail_in[s], 16)
                sp.dma_start(tail_x[s], x2_scr[s, :, :]).then_inc(tail_in[s], 16)
            with sp.Fori(1, NB // 4) as it:
                for s in range(4):
                    sp.wait_ge(tail_out[s], 16 * it)
                    sp.dma_start(tail_z[s], z_scr[4 * it + s, :, :]).then_inc(tail_in[s], 16)
                    sp.dma_start(tail_x[s], x2_scr[4 * it + s, :, :]).then_inc(tail_in[s], 16)
            for s in range(4):
                sp.wait_ge(tail_out[s], 16 * (NB // 4))

        @block.gpsimd
        def _(pool):
            pool.memset(ones[:, :], 1.0).then_inc(consts_made, 1)
            pool.memset(neg_half[:, :], -0.5).then_inc(consts_made, 1)
            pool.memset(count_start[:, 0:1], 0.0).then_inc(x2_out, 16)
            pool.memset(count_start[:, 1:2], 0.0).then_inc(z_out, 16)
            pool.memset(rms_eps[:, :], EPS * KEEP ** -2).then_inc(consts_made, 1)

            def pair(u, g, q):
                pool.wait_ge(exp_done, 64 * u + 4 * q + 4)
                if g == 1 or q > 0:
                    pool.wait_ge(sum_done, 16 * u + q)
                a = 2 * q
                pool.tensor_tensor(pair_sum[:, :, :], probs[a % 4][:, :, :],
                                   probs[(a + 1) % 4][:, :, :], ALU.add).then_inc(pair_added, 1)

            def inv_sqrt(n):
                pool.wait_ge(ln_stat, LN_STEPS * (n + 1))
                pool.tensor_tensor(rstd[:, :], var_eps[:, :], neg_half[:, :], ALU.pow)\
                    .then_inc(ln_pow, 1)

            def iteration(b, last):
                for g in range(G):
                    for q in range(4 * ROUNDS):
                        pair(2 * b + g, g, q)
                inv_sqrt(2 * b + 2)
                if not last:
                    inv_sqrt(2 * b + 3)

            pool.wait_ge(consts_made, 7)
            inv_sqrt(0)
            inv_sqrt(1)
            with pool.Fori(0, NB - 1) as b:
                iteration(b, False)
            iteration(NB - 1, True)
            with pool.Fori(0, NB // 4) as it:
                for s in range(4):
                    pool.wait_ge(tail_tanh, 4 * it + s + 1)
                    pool.tensor_tensor(tail_x[s], tail_x[s], tail_z[s], ALU.add)\
                        .then_inc(tail_sum, 1)
                    pool.wait_ge(tail_sum, 4 * it + s + 1)
                    pool.dma_start(out[4 * it + s, :, :], tail_x[s]).then_inc(tail_out[s], 16)

        @block.scalar
        def _(act):
            act.wait_ge(consts_made, 7)
            act.wait_ge(lam_step, 4)
            act.activation(lam_exp[:, :], lam_dot[:, :], ACT.Exp).then_inc(lam_step, 1)

            def take(rb, i, dst, func=ACT.Copy, **kw):
                act.wait_ge(ring_ready, rb + i + 1)
                act.activation(dst, ring(i), func, **kw).then_inc(act_out, 1)

            def take_xt(n):
                for h in range(2):
                    for c in range(KC):
                        act.wait_ge(xt_ready, 4 * n + (2 * h + c + 1))
                        act.activation(xt[:, c, h * HALF:(h + 1) * HALF], xt_ps[c][:, :],
                                       ACT.Copy).then_inc(xt_out, 1)

            def take_qk(rb, u, g):
                for X in range(2):
                    if g == 1:
                        act.wait_ge(rope_done, 2 * u - 1 + X)
                    for h in range(2):
                        take(rb, (QK1 if g else QK0) + 2 * X + h,
                             raw[X][:, h * HALF:(h + 1) * HALF])

            def take_v(rb, js):
                for j in js:
                    take(rb, VAL + j, values[:, 2 * j:2 * j + 2, :].rearrange("p a b -> p (a b)"))

            def copy_o(u, g, r):
                if g == 1 or r > 1:
                    act.wait_ge(at_ready, 2 * u + r // 2)
                act.wait_ge(av_done, 32 * u + 8 * (r + 1))
                act.activation(o_copy[:, r % 2, :], o_ps[:, :], ACT.Copy).then_inc(o_read, 1)

            def copy_sums(u, g, r):
                if g == 1 or r > 0:
                    act.wait_ge(o_scaled, 4 * u + r)
                act.wait_ge(sum_done, 16 * u + 4 * (r + 1))
                act.activation(inv_sum[:, :], sum_ps[:, :], ACT.Copy).then_inc(sum_read, 1)

            def exps(u, g):
                for kk in range(STEPS):
                    if g == 1 or kk >= 4:
                        act.wait_ge(av_done, 32 * u + (kk - 3))
                        act.wait_ge(pair_added, 16 * u + (kk // 2 - 1))
                    for hp in range(2):
                        act.wait_ge(st_ready, 64 * u + (2 * kk + hp + 1))
                        act.activation(probs[kk % 4][:, 2 * hp:2 * hp + 2, :], st[hp][:, :, :],
                                       ACT.Exp).then_inc(exp_done, 1)
                    if kk % 8 == 0 and kk:
                        copy_o(u, g, kk // 8 - 1)
                    if kk % 8 == 3 and kk > 8:
                        copy_sums(u, g, kk // 8 - 1)
                copy_o(u, g, 3)

            def iteration(b, last):
                rb, ab = ring_base(b, last), act_base(b, last)
                if not last:
                    take_xt(2 * b + 1)
                    take_qk(rb, 2 * b + 2, 0)
                act.wait_ge(x2_out, 16 * b + 16)
                act.wait_ge(z_out, 16 * b + 16)
                act.wait_ge(cell_ready, 4 * b + 1)
                exps(2 * b, 0)
                if not last:
                    take_qk(rb, 2 * b + 3, 1)
                copy_sums(2 * b, 0, 3)
                exps(2 * b + 1, 1)
                if not last:
                    take_v(rb, (0, 1))
                copy_sums(2 * b + 1, 1, 3)
                if not last:
                    take_v(rb, (2, 3))
                for i in range(4):
                    take(rb, RMS + i, rms[:, i, :], ACT.Ln, scale=KEEP ** -2 / (2 * D),
                         bias=rms_eps[:, 0:1])
                for i in range(4):
                    act.wait_ge(act_out, ab + (RMS + i + 1))
                    act.activation(rms[:, i, :], rms[:, i, :], ACT.Exp, scale=-0.5)\
                       .then_inc(rms_inv, 1)
                take_xt(2 * b + (1 if last else 2))
                for h in range(2):
                    for m in range(KC):
                        if h == 1:
                            act.wait_ge(cell_ready, 4 * b + (2 + m))
                        for a, func in enumerate((ACT.Sigmoid, ACT.Sigmoid, ACT.Tanh)):
                            take(rb, GATE + 6 * h + 3 * m + a, gates[m][:, a, :], func,
                                 bias=gate_bias[:, a, m:m + 1])
                for j in range(4):
                    take(rb, ZED + j, zed[:, 2 * j * E:2 * (j + 1) * E])

            act.wait_ge(consts_in, N_CONST)
            take_xt(0)
            take_qk(0, 0, 0)
            take_qk(0, 1, 1)
            take_v(0, range(4))
            with act.Fori(0, NB - 1) as b:
                iteration(b, False)
            iteration(NB - 1, True)
            rb = ring_base(NB - 1, True)
            act.wait_ge(x2_out, 16 * (NB + 1))
            for j in range(4):
                take(rb, GEE + j, x2[:, 2 * j * E:2 * (j + 1) * E])
            with act.Fori(0, NB // 4) as it:
                for s in range(4):
                    act.wait_ge(tail_add, 4 * it + s + 1)
                    act.activation(tail_z[s], tail_z[s], ACT.Tanh).then_inc(tail_tanh, 1)

        @block.tensor
        def _(pe):
            def turn(i, b, ab):
                p = i - 4
                if WO <= p < WO + 4:
                    pe.wait_ge(wo_added, 4 * b + (p - WO + 1))
                elif not (isinstance(ab, int) and ab + p + 1 <= 0):
                    pe.wait_ge(act_out, ab + (act_index(p) + 1))

            def transposes(src, ln_out, m, n):
                for h in range(2):
                    pe.wait_ge(ln_out, TT * m + (4 * h + 4))
                    for c in range(KC):
                        if h == 1:
                            pe.wait_ge(xt_out, 4 * n + (c + 1))
                        for t in range(4):
                            at = (4 * h + t) * E + c * P
                            mm = pe.transpose(xt_ps[c][:, t * P:(t + 1) * P], src[:, at:at + P],
                                              ident[:, :])
                        mm.then_inc(xt_ready, 1)

            def qk(g, b, ab):
                for X in range(2):
                    for h in range(2):
                        i = (QK1 if g else QK0) + 2 * X + h
                        turn(i, b, ab)
                        for c in range(KC):
                            mm = pe.matmul(ring(i), weights[:, W_Q + X, c, g * P:(g + 1) * P],
                                           xt[:, c, h * HALF:(h + 1) * HALF],
                                           start=(c == 0), stop=(c == KC - 1))
                        mm.then_inc(ring_ready, 1)

            def rows_out(first, w, src, b, ab, bias=False, js=range(4), beside=(0, 0, iter(()))):
                un, un_group, blocks = beside
                for j in js:
                    i = first + j
                    turn(i, b, ab)
                    for t in range(2):
                        dst = ring(i)[:, t * E:(t + 1) * E]
                        at = (2 * j + t) * P
                        for c in range(KC):
                            mm = pe.matmul(dst, src[:, c, at:at + P], weights[:, w, c, :],
                                           start=(c == 0), stop=(c == KC - 1 and not bias))
                            for n in itertools.islice(blocks, 1):
                                score(un, un_group, n)
                        if bias:
                            mm = pe.matmul(dst, ones[0:1, :], bo_row[:, :], start=False,
                                           stop=True)
                    mm.then_inc(ring_ready, 1)

            def score(u, g, i):
                s, t, h = i // 16, i % 16 // 2, i % 2
                if i >= 2:
                    pe.wait_ge(max_done, SCORES * u + (i - 1))
                pe.matmul(s_ps[i % 2][:, :], q_stack[g][0:SROWS, s, t * P:(t + 1) * P],
                          k_stack[g][0:SROWS, s, h * HALF:(h + 1) * HALF],
                          start=True, stop=True).then_inc(score_ready, 1)

            def score_start(u):
                pe.wait_ge(stack_in[0], 16 * BLK * (u + 1))
                pe.wait_ge(stack_in[1], 16 * BLK * (u + 1))
                if not (isinstance(u, int) and u == 0):
                    pe.wait_ge(shift_made, u)

            def turn_max(u):
                pe.wait_ge(max_all, u + 1)
                pe.transpose(s_ps[0][:, 0:P], neg_max[:, :], ident[:, :])\
                    .then_inc(max_turned, 1)

            def key_tile(u, g, kk, hp):
                th, sub, kt = kk // 16, kk // 8 % 2, kk % 8
                if kk >= 1:
                    pe.wait_ge(exp_done, 64 * u + (2 * kk + hp - 1))
                for j in range(2):
                    s = 2 * (2 * hp + j) + sub
                    mm = pe.matmul(st[hp][:, j, :],
                                   k_stack[g][0:KROWS, s, kt * P:(kt + 1) * P],
                                   q_stack[g][0:KROWS, s, th * HALF:(th + 1) * HALF],
                                   start=True, stop=True)
                mm.then_inc(st_ready, 1)

            def weighted(u, g, kk):
                r, kt = kk // 8, kk % 8
                pe.wait_ge(exp_done, 64 * u + (2 * kk + 2))
                if kt == 0 and (g == 1 or r > 0):
                    pe.wait_ge(o_read, 4 * u + r)
                for h in range(4):
                    at = (4 * g + h) * 2 * D
                    mm = pe.matmul(o_ps[32 * h:32 * h + 32, :], values[:, kt, at:at + 2 * D],
                                   probs[kk % 4][:, h, :], start=(kt == 0), stop=(kt == KT - 1))
                mm.then_inc(av_done, 1)

            def key_sums(u, g, q):
                r, p = q // 4, q % 4
                pe.wait_ge(pair_added, 16 * u + (q + 1))
                if p == 0 and (g == 1 or r > 0):
                    pe.wait_ge(sum_read, 4 * u + r)
                for h in range(4):
                    mm = pe.matmul(sum_ps[32 * h:32 * h + 32, :], ones[:, 0:32],
                                   pair_sum[:, h, :], start=(p == 0), stop=(p == 3))
                mm.then_inc(sum_done, 1)

            def attention(u, g, un, plan):
                pe.wait_ge(shift_in, 48 * (u + 1))
                for s in range(STEPS):
                    todo = list(plan[s])
                    key_tile(u, g, s, 0)
                    if todo and todo[0] == 0:
                        score_start(un)
                    for i in todo[0:1]:
                        score(un, 1 - g, i)
                    key_tile(u, g, s, 1)
                    for i in todo[1:2]:
                        score(un, 1 - g, i)
                    if s >= 1:
                        weighted(u, g, s - 1)
                    for i in todo[2:3]:
                        score(un, 1 - g, i)
                    if s >= 4 and s % 2 == 0:
                        key_sums(u, g, (s - 4) // 2)
                    for i in todo[3:]:
                        score(un, 1 - g, i)
                weighted(u, g, STEPS - 1)
                key_sums(u, g, 14)

            def iteration(b, last):
                ab = act_base(b, last)
                u = 2 * b
                if not last:
                    transposes(xa, ln1_out, b + 1, 2 * b + 1)
                    pe.wait_ge(xt_out, 4 * (2 * b + 2))
                    qk(0, b, ab)
                    pe.wait_ge(act_out, ab + QK0 + 4)
                else:
                    pe.wait_ge(act_out, ab + PRE)
                attention(u, 0, u + 1, PLAN0)
                turn_max(u + 1)
                if not last:
                    qk(1, b, ab)
                key_sums(u, 0, 15)
                if not last:
                    pe.wait_ge(act_out, ab + QK1 + 4)
                attention(u + 1, 1, u + 2, NO_PLAN if last else PLAN1)
                late = iter(range(SCORES - sum(LATE), SCORES))
                if not last:
                    rows_out(VAL, W_V, xt, b, ab, js=(0, 1),
                             beside=(u + 2, 0, itertools.islice(late, LATE[0])))
                key_sums(u + 1, 1, 15)
                if not last:
                    rows_out(VAL, W_V, xt, b, ab, js=(2, 3))
                for i in range(4):
                    pe.wait_ge(sq_ready, 4 * b + (i + 1))
                    turn(RMS + i, b, ab)
                    pe.matmul(ring(RMS + i), head_ones[:, :], square[:, i, :], start=True,
                              stop=True).then_inc(ring_ready, 1)
                if not last:
                    for i in late:
                        score(u + 2, 0, i)
                    turn_max(u + 2)
                pe.wait_ge(at_norm, 4 * b + 4)
                rows_out(WO, W_O, attn_t, b, ab)
                early = iter(()) if last else iter(range(sum(EARLY)))

                def gate_part(i, cell, start, stop):
                    h, m, a = i // 6, i % 6 // 3, i % 3
                    hs, ms = slice(h * HALF, (h + 1) * HALF), slice(m * P, (m + 1) * P)
                    for c in range(KC):
                        mm = pe.matmul(ring(GATE + i),
                                       weights[:, (U_F if cell else W_F) + a, c, ms],
                                       (cell_t if cell else xt)[:, c, hs],
                                       start=(start and c == 0), stop=(stop and c == KC - 1))
                        if i in (4, 5, 6) or i >= 8:
                            for n in itertools.islice(early, 1):
                                if n == 0:
                                    score_start(u + 3)
                                score(u + 3, 1, n)
                    return mm

                pe.wait_ge(cell_ready, 4 * b + 1)
                for i in range(4):
                    turn(GATE + i, b, ab)
                    gate_part(i, True, True, False)
                transposes(xn2, ln2_out, b, 2 * b + (1 if last else 2))
                pe.wait_ge(xt_out, 4 * (2 * b + (2 if last else 3)))
                for i in range(4):
                    gate_part(i, False, False, True).then_inc(ring_ready, 1)
                for i in range(4, 12):
                    turn(GATE + i, b, ab)
                    gate_part(i, True, True, False)
                    gate_part(i, False, False, True).then_inc(ring_ready, 1)
                rows_out(ZED, W_Z, xt, b, ab, js=(0, 1))
                rows_out(ZED, W_Z, xt, b, ab, js=(2, 3), beside=(u + 3, 1, early))
                assert not list(early)

            pe.wait_ge(consts_in, N_CONST)
            pe.wait_ge(consts_made, 7)
            transposes(xa, ln1_out, 0, 0)
            pe.wait_ge(xt_out, 4)
            qk(0, 0, 0)
            qk(1, 0, 0)
            rows_out(VAL, W_V, xt, 0, 0)
            score_start(0)
            for i in range(SCORES):
                score(0, 0, i)
            turn_max(0)
            score_start(1)
            for i in range(sum(EARLY)):
                score(1, 1, i)
            with pe.Fori(0, NB - 1) as b:
                iteration(b, False)
            iteration(NB - 1, True)
            pe.wait_ge(cell_ready, 4 * NB + 1)
            pe.wait_ge(uo_in, 16)
            rows_out(GEE, U_Z, cell_t, NB - 1, act_base(NB - 1, True), bias=True)

        @block.vector
        def _(dve):
            def norm_stats(n, src):
                for t in range(TT):
                    dve.bn_stats(stats[:, t, :], src[:, t * E:(t + 1) * E]).then_inc(ln_stat, 1)
                even, odd = stats[:, :, 0:3], stats[:, :, 3:6]
                dve.wait_ge(ln_stat, LN_STEPS * n + TT)
                dve.tensor_tensor(ln_sum[:, :], even[:, :, 1], odd[:, :, 1], ALU.add)\
                   .then_inc(ln_stat, 1)
                dve.tensor_tensor(ln_diff[:, :], even[:, :, 1], odd[:, :, 1], ALU.subtract)\
                   .then_inc(ln_stat, 1)
                dve.tensor_tensor(ln_square[:, :], even[:, :, 2], odd[:, :, 2], ALU.add)\
                   .then_inc(ln_stat, 1)
                dve.wait_ge(ln_stat, LN_STEPS * n + TT + 3)
                dve.tensor_scalar(mean[:, :], ln_sum[:, :], 0.5, None, ALU.mult)\
                   .then_inc(ln_stat, 1)
                dve.scalar_tensor_tensor(out=ln_between[:, :], in0=ln_diff[:, :], scalar=0.25,
                                         in1=ln_diff[:, :], op0=ALU.mult, op1=ALU.mult)\
                   .then_inc(ln_stat, 1)
                dve.tensor_scalar(ln_square[:, :], ln_square[:, :], 1.0 / E, EPS, ALU.mult,
                                  ALU.add).then_inc(ln_stat, 1)
                dve.wait_ge(ln_stat, LN_STEPS * n + TT + 6)
                dve.tensor_tensor(var_eps[:, :], ln_square[:, :], ln_between[:, :], ALU.add)\
                   .then_inc(ln_stat, 1)

            def normalise(n, src, dst, ln_out):
                dve.wait_ge(ln_pow, n + 1)
                for t in range(TT):
                    dve.tensor_scalar(dst[:, t * E:(t + 1) * E], src[:, t * E:(t + 1) * E],
                                      mean[:, t:t + 1], rstd[:, t:t + 1], ALU.subtract,
                                      ALU.mult).then_inc(ln_out, 1)

            def rope(u, steps=range(14)):
                for X, k in (divmod(step, 7) for step in steps):
                    n = 2 * u + X
                    if k == 0:
                        dve.wait_ge(swap_in[X], 32 * (u + 1))
                        dve.tensor_tensor(raw[X], raw[X], rope_tab[:, 2 * X, :], ALU.mult)\
                           .then_inc(rope_step, 1)
                    if k == 1:
                        dve.tensor_tensor(swapped[:, X, :], swapped[:, X, :],
                                          rope_tab[:, 2 * X + 1, :], ALU.mult)\
                           .then_inc(rope_step, 1)
                    if k == 2:
                        dve.wait_ge(rope_step, 6 * n + 2)
                        dve.tensor_tensor(raw[X], raw[X], swapped[:, X, :], ALU.add)\
                           .then_inc(rope_step, 1)
                    if k == 3:
                        dve.wait_ge(rope_step, 6 * n + 3)
                        if not (isinstance(n, int) and n == 0):
                            dve.wait_ge(parts_out, 16 * n)
                        dve.tensor_copy(parts[:, 0, :], raw[X]).then_inc(rope_step, 1)
                    if k == 4:
                        dve.wait_ge(rope_step, 6 * n + 4)
                        dve.tensor_tensor(swapped[:, X, :], raw[X], parts[:, 0, :],
                                          ALU.subtract).then_inc(rope_step, 1)
                    if k == 5:
                        dve.wait_ge(rope_step, 6 * n + 5)
                        dve.tensor_copy(parts[:, 1, :], swapped[:, X, :]).then_inc(rope_step, 1)
                    if k == 6:
                        dve.wait_ge(rope_step, 6 * n + 6)
                        dve.tensor_tensor(parts[:, 2, :], swapped[:, X, :], parts[:, 1, :],
                                          ALU.subtract).then_inc(rope_done, 1)

            def maximum(u, i):
                dve.wait_ge(score_ready, SCORES * u + (i + 1))
                dve.tensor_reduce(neg_max2[:, i // 2, i % 2:i % 2 + 1], s_ps[i % 2][:, :], AX.X,
                                  ALU.max, negate=True).then_inc(max_done, 1)

            def join_max(u):
                dve.wait_ge(max_done, SCORES * (u + 1))
                dve.tensor_reduce(neg_max[:, 0:SUBS * TT], neg_max2[:, :, :], AX.X, ALU.min)\
                   .then_inc(max_all, 1)

            def split_shift(u):
                src = s_ps[0][0:SUBS * TT, 0:P]
                dve.wait_ge(max_turned, u + 1)
                if not (isinstance(u, int) and u == 0):
                    dve.wait_ge(shift_in, 48 * u)
                dve.tensor_copy(shift[:, 0, :], src).then_inc(shift_step, 1)
                dve.wait_ge(shift_step, 3 * u + 1)
                dve.tensor_tensor(shift_rest[:, :], src, shift[:, 0, :], ALU.subtract)\
                   .then_inc(shift_step, 1)
                dve.wait_ge(shift_step, 3 * u + 2)
                dve.tensor_copy(shift[:, 1, :], shift_rest[:, :]).then_inc(shift_step, 1)
                dve.wait_ge(shift_step, 3 * u + 3)
                dve.tensor_tensor(shift[:, 2, :], shift_rest[:, :], shift[:, 1, :],
                                  ALU.subtract).then_inc(shift_made, 1)

            def invert_sums(u, r, part):
                if part == 0:
                    dve.wait_ge(sum_read, 4 * u + (r + 1))
                cols = inv_sum[:, part * P:(part + 1) * P]
                dve.reciprocal(cols, cols).then_inc(sum_inv, 1)

            def divide(u, g, r):
                dve.wait_ge(sum_inv, 16 * u + 4 * (r + 1))
                dve.wait_ge(o_read, 4 * u + (r + 1))
                dve.tensor_tensor(o_copy[:, r % 2, :], o_copy[:, r % 2, :], inv_sum[:, :],
                                  ALU.mult).then_inc(o_scaled, 1)
                if r % 2 == 1:
                    th = r // 2
                    dve.wait_ge(o_scaled, 4 * u + (r + 1))
                    dve.scalar_tensor_tensor(out=attn_t[:, g, th * HALF:(th + 1) * HALF],
                                             in0=o_copy[:, 1, :], scalar=neg_lam[:, 0:1],
                                             in1=o_copy[:, 0, :], op0=ALU.mult, op1=ALU.add)\
                       .then_inc(at_ready, 1)

            def attention(u, g, un, plan, turned=None):
                for s in range(STEPS):
                    for i in plan[s]:
                        maximum(un, i)
                    if turned is not None and 3 <= s < 17:
                        rope(turned, [s - 3])
                    if s > 8 and 3 <= s % 8 <= 6:
                        invert_sums(u, s // 8 - 1, s % 8 - 3)
                    if s > 8 and s % 8 == 7:
                        divide(u, g, s // 8 - 1)

            def iteration(b, last):
                rb, ab = ring_base(b, last), act_base(b, last)
                u = 2 * b
                attention(u, 0, u + 1, PLAN0, None if last else u + 2)
                join_max(u + 1)
                split_shift(u + 1)
                for k in range(4):
                    invert_sums(u, 3, k)
                divide(u, 0, 3)
                attention(u + 1, 1, u + 2, NO_PLAN if last else PLAN1,
                          None if last else u + 3)
                late, early = iter(range(SCORES - sum(LATE), SCORES)), iter(range(sum(EARLY)))
                if not last:
                    for i in itertools.islice(late, LATE[0]):
                        maximum(u + 2, i)
                for k in range(4):
                    invert_sums(u + 1, 3, k)
                divide(u + 1, 1, 3)
                for i in range(4):
                    g, th = i // 2, i % 2
                    part = attn_t[:, g, th * HALF:(th + 1) * HALF]
                    dve.wait_ge(at_ready, 4 * b + (i + 1))
                    dve.tensor_tensor(square[:, i, :], part, part, ALU.mult).then_inc(sq_ready, 1)
                if not last:
                    for i in late:
                        maximum(u + 2, i)
                    join_max(u + 2)
                for i in range(4):
                    g, th = i // 2, i % 2
                    part = attn_t[:, g, th * HALF:(th + 1) * HALF]
                    dve.wait_ge(rms_inv, 4 * b + (i + 1))
                    dve.tensor_tensor(part, part, rms[:, i, :], ALU.mult).then_inc(at_norm, 1)
                if not last:
                    split_shift(u + 2)
                dve.wait_ge(xr_in, 16 * (b + 1))
                for j in range(4):
                    rows = x2[:, 2 * j * E:2 * (j + 1) * E]
                    dve.wait_ge(ring_ready, rb + (WO + j + 1))
                    dve.tensor_tensor(rows, ring(WO + j), rows, ALU.add).then_inc(wo_added, 1)
                dve.wait_ge(wo_added, 4 * b + 4)
                norm_stats(u + 2, x2)
                normalise(u + 2, x2, xn2, ln2_out)
                if not last:
                    dve.wait_ge(x_in, 16 * b + 48)
                    norm_stats(u + 3, xa)
                    normalise(u + 3, xa, xa, ln1_out)
                    for i in itertools.islice(early, EARLY[0]):
                        maximum(u + 3, i)
                cells(b, ab, 0)
                if not last:
                    for i in itertools.islice(early, EARLY[1]):
                        maximum(u + 3, i)
                cells(b, ab, 1)
                if not last:
                    for i in early:
                        maximum(u + 3, i)

            def cells(b, ab, h):
                dve.wait_ge(act_out, ab + (act_index(GATE) + 6 * h + 6))
                for m in range(KC):
                    f, i, a = (gates[m][:, j, :] for j in range(3))
                    c = cell_t[:, m, h * HALF:(h + 1) * HALF]
                    dve.tensor_tensor(i, i, a, ALU.mult).then_inc(cell_step, 1)
                    dve.tensor_tensor(f, f, c, ALU.mult).then_inc(cell_step, 1)
                    dve.wait_ge(cell_step, 8 * b + (4 * h + 2 * m + 2))
                    dve.tensor_tensor(c, f, i, ALU.add).then_inc(cell_ready, 1)

            dve.memset(head_ones[:, :], 0.0).then_inc(lam_step, 1)
            dve.wait_ge(lam_step, 1)
            for h in range(4):
                mm = dve.memset(head_ones[32 * h:32 * h + 32, 32 * h:32 * h + 32], 1.0)
            mm.then_inc(consts_made, 1)
            for g in range(G):
                dve.memset(k_stack[g][SROWS:P, :, :], 1.0).then_inc(consts_made, 1)
            dve.wait_ge(x_in, 16)
            norm_stats(0, xa)
            dve.wait_ge(consts_in, N_CONST)
            for a in range(2):
                dve.tensor_tensor(lam_prod[:, a, :], lam_in[:, 2 * a, :], lam_in[:, 2 * a + 1, :],
                                  ALU.mult).then_inc(lam_step, 1)
            dve.wait_ge(lam_step, 3)
            dve.tensor_reduce(lam_dot[:, :], lam_prod[:, :, :], AX.X, ALU.add)\
               .then_inc(lam_step, 1)
            dve.memset(neg_max[:, SUBS * TT:P], 0.0)
            dve.memset(cell_t[:, :, :], 0.0).then_inc(consts_made, 1)
            dve.wait_ge(consts_made, 7)
            for c in range(KC):
                mm = dve.tensor_scalar(cell_t[:, c, :], cell_t[:, c, :], cell0[:, c:c + 1], None,
                                       ALU.add)
            mm.then_inc(cell_ready, 1)
            normalise(0, xa, xa, ln1_out)
            dve.wait_ge(lam_step, 5)
            dve.tensor_tensor(neg_lam[:, :], lam_exp[:, 1:2], lam_exp[:, 0:1], ALU.subtract)\
               .then_inc(lam_step, 1)
            dve.wait_ge(lam_step, 6)
            dve.tensor_scalar(neg_lam[:, :], neg_lam[:, :], -LAMBDA_INIT, None, ALU.add)\
               .then_inc(lam_step, 1)
            rope(0)
            rope(1)
            for i in range(SCORES):
                maximum(0, i)
            join_max(0)
            split_shift(0)
            dve.wait_ge(x_in, 32)
            norm_stats(1, xa)
            normalise(1, xa, xa, ln1_out)
            for i in range(sum(EARLY)):
                maximum(1, i)
            dve.wait_ge(lam_step, 7)
            with dve.Fori(0, NB - 1) as b:
                iteration(b, False)
            iteration(NB - 1, True)
            dve.wait_ge(act_out, act_base(NB - 1, True) + act_index(GEE) + 4)
            with dve.Fori(0, NB // 4) as it:
                for s in range(4):
                    dve.wait_ge(tail_in[s], 32 * it + 32)
                    dve.tensor_tensor(tail_z[s], tail_z[s], x2, ALU.add).then_inc(tail_add, 1)


def rope_tables():
    f32 = np.float32
    even = np.arange(0, D, 2, dtype=f32)
    inv_freq = f32(1.0) / np.power(f32(10000.0), even / f32(D), dtype=f32)
    pos = np.arange(T, dtype=f32)
    freqs = np.repeat(pos[:, None] * inv_freq[None, :], 2, axis=-1).astype(np.float64)
    sv = (even + f32(0.4 * D)) / f32(1.4 * D)
    power = (pos - T // 2) / f32(512.0)
    scale = np.power(sv[None, :].astype(np.float64), power[:, None].astype(np.float64))
    scale = np.concatenate([scale, scale], axis=-1)
    cos, sin = np.cos(freqs), np.sin(freqs)
    sin[:, 0::2] *= -1.0
    q, k = scale * D ** -0.5, 1.0 / scale
    token = (np.arange(P)[None, :] * TT + np.arange(TT)[:, None]).reshape(-1)
    tabs = [np.tile(a[token].T, (SUBS, 1)) for a in (cos * q, sin * q, cos * k, sin * k)]
    return np.ascontiguousarray(np.stack(tabs).astype(f32))


_NAMES = ["attn_Wq", "attn_Wk", "attn_Wv", "attn_Wo", "attn_lambda_q1", "attn_lambda_k1",
          "attn_lambda_q2", "attn_lambda_k2", "ffn_wf", "ffn_uf", "ffn_bf", "ffn_wi", "ffn_ui",
          "ffn_bi", "ffn_wc", "ffn_uc", "ffn_bc", "ffn_wo", "ffn_uo", "ffn_bo", "ffn_in_c"]


def kernel(**inputs):
    import concourse.bacc as _bacc
    from concourse.bass_utils import run_bass_kernel_spmd as _run

    nc = _bacc.Bacc("TRN2", target_bir_lowering=False, num_devices=1)
    arrays = {"x": np.ascontiguousarray(inputs["L0_attn_x"]).reshape(NB, P, TT * E)}
    for name in _NAMES:
        a = np.asarray(inputs["L0_" + name])
        if name in ("ffn_bf", "ffn_bi", "ffn_bc", "ffn_in_c"):
            a = a.reshape(KC, P)
        arrays[name] = np.ascontiguousarray(a.T)
    arrays["rope_tables"] = rope_tables()
    arrays["identity"] = np.eye(P, dtype=np.float32)
    args = [nc.dram_tensor("in_" + n, a.shape, mybir.dt.from_np(a.dtype),
                           kind="ExternalInput").ap() for n, a in arrays.items()]
    out = nc.dram_tensor("out_rows", (NB, P, TT * E), F32, kind="ExternalOutput").ap()
    build(nc, *args, out)
    r = _run(nc, [{"in_" + n: a for n, a in arrays.items()}], core_ids=[0])
    return r.results[0]["out_rows"].reshape(NB, T, E)
```

```python
import itertools
import math
from contextlib import ExitStack

import numpy as np

import concourse.bass as bass
from concourse import mybir

ALU = mybir.AluOpType
ACT = mybir.ActivationFunctionType
AX = mybir.AxisListType
F32 = mybir.dt.float32
BF16 = mybir.dt.bfloat16

P = 128
NB, T, E = 16, 1024, 256
H = 8
D = E // H // 2
TT = T // P
KC = E // P
HALF = T // 2
G = 2
SUBS = 8
BLK = 6
SROWS = BLK * D
KROWS = SROWS + 3
Q_PART = (0, 0, 1, 1, 0, 2)
K_PART = (0, 1, 0, 1, 2, 0)
LAMBDA_INIT = 0.8 - 0.6 * math.exp(-0.3 * 1)
KEEP = 1.0 - LAMBDA_INIT
EPS = 1e-5

QK0, QK1, WO, GATE, ZED, GEE = 0, 4, 16, 20, 32, 36
VAL = (8, 9, 13, 14)
RMS = (10, 11, 12, 15)
LAST_RMS = (12, 13, 14, 15)
PER_ITER = 36
PRE = 12
ACT_ITER = PER_ITER - 4

ROUNDS, KT = 4, 8
STEPS = ROUNDS * KT
LN_STEPS = TT + 7
SCORES = SUBS * TT * 2


def act_index(i):
    return i if i < WO else i - 4


LATE = (8, 3, 5, 4, 12)
EARLY = (16, 12, 8)
BEFORE = EARLY[0] + EARLY[1]
ROPE_AT = (1, 2, 3, 4, 5, 6, 7, 8, 9, 10, 16, 17, 18, 24)
SUM_STEP = 1.4
WORK = [(1.9, 1.9, 1.9, 1, 1.9, 1, 1.9)[ROPE_AT.index(s) % 7] if s in ROPE_AT else 0
        for s in range(STEPS)]
for s in range(9, STEPS):
    WORK[s] += (0, 0, 0, 1.5, 1.5, 1.5, 1.5, 1)[s % 8]


def score_plan(first, last, start):
    room = [0 if s < start else SUM_STEP if s % 2 == 0 and s >= 4 else 1 for s in range(STEPS)]
    work = [w * (s >= start) for s, w in enumerate(WORK)]
    per_room = (last - first + sum(work)) / sum(room)
    plan, at, due = [], first, 0.0
    for s in range(STEPS):
        due += room[s] * per_room - work[s]
        n = max(0, min(int(due), last - at))
        if s == STEPS - 1:
            n = last - at
        due -= n
        plan.append(range(at, at + n))
        at += n
    return plan


PLAN0 = score_plan(sum(EARLY), SCORES, 0)
PLAN1 = score_plan(0, SCORES - sum(LATE), 3)
NO_PLAN = [range(0)] * STEPS


def build(nc, x, wq, wk, wv, wo_attn, lq1, lk1, lq2, lk2, wf, uf, bf, wi, ui, bi, wc, uc, bc,
          wo, uo, bo, in_c, tables, ident_in, out):
    qk_scr = nc.dram_tensor("qk_parts", (2, 3, P, T), BF16, kind="Internal").ap()
    x2_scr = nc.dram_tensor("x2_rows", (NB, P, TT * E), F32, kind="Internal").ap()
    z_scr = nc.dram_tensor("z_rows", (NB, P, TT * E), F32, kind="Internal").ap()

    with ExitStack() as ctx:
        def sb(name, shape, dt=F32):
            return ctx.enter_context(nc.sbuf_tensor(name, shape, dt))

        def sem(name):
            return ctx.enter_context(nc.semaphore(name))

        q_stack = [sb(f"q_stack{g}", [P, SUBS, T], BF16) for g in range(G)]
        k_stack = [sb(f"k_stack{g}", [P, SUBS, T], BF16) for g in range(G)]
        weights = sb("weights", [P, 11, KC, E])
        W_Q, W_K, W_V, W_O, W_F, W_I, W_C, U_F, U_I, U_C, W_Z = range(11)
        U_Z = W_Q
        rope_tab = sb("rope_tab", [P, 4, T])
        values = sb("values", [P, TT, E])
        probs = [sb(f"probs{i}", [P, 4, HALF]) for i in range(4)]
        pair_sum = sb("pair_sum", [P, 4, HALF])
        xa = sb("xa", [P, TT * E])
        xt = sb("xt", [P, KC, T])
        swapped = sb("swapped", [P, 2, T])
        parts = sb("parts", [P, 3, T], BF16)
        attn_t = sb("attn_t", [P, G, T])
        o_copy = sb("o_copy", [P, 2, HALF])
        inv_sum = sb("inv_sum", [P, HALF])
        cell_t = sb("cell_t", [P, KC, T])
        ident = sb("ident", [P, P])
        head_ones = sb("head_ones", [P, P])
        ones = sb("ones", [P, P])
        gate_bias = sb("gate_bias", [P, 3, KC])
        cell0 = sb("cell0", [P, KC])
        bo_row = sb("bo_row", [1, E])
        lam_in = sb("lam_in", [P, 4, D])
        lam_prod = sb("lam_prod", [P, 2, D])
        lam_dot = sb("lam_dot", [P, 2])
        lam_exp = sb("lam_exp", [P, 2])
        neg_lam = sb("neg_lam", [P, 1])
        rms_eps = sb("rms_eps", [P, 1])
        neg_half = sb("neg_half", [P, TT])
        count_start = sb("count_start", [P, 2])
        stats = sb("stats", [P, TT, 6])
        ln_sum, ln_diff, ln_square, ln_between, mean = (
            sb(n, [P, TT]) for n in ("ln_sum", "ln_diff", "ln_square", "ln_between", "mean"))
        var_eps = sb("var_eps", [P, TT])
        rstd = sb("rstd", [P, TT])
        neg_max2 = sb("neg_max2", [P, SUBS * TT, 2])
        neg_max = sb("neg_max", [P, P])
        shift_rest = sb("shift_rest", [SUBS * TT, P])
        shift = sb("shift", [SUBS * TT, 3, P], BF16)

        raw = [xa[:, 0:T], xa[:, T:2 * T]]
        x2 = probs[0][:, :, :].rearrange("p a b -> p (a b)")
        xn2 = probs[1][:, :, :].rearrange("p a b -> p (a b)")
        zed = xn2
        rms = probs[1]
        square = probs[1]
        gates = [probs[2], probs[3]]

        st = [ctx.enter_context(nc.psum_tensor(f"st{i}", [P, 2, HALF], F32)) for i in range(2)]
        s_ps = [ctx.enter_context(nc.psum_tensor(f"s_ps{i}", [P, HALF], F32)) for i in range(2)]
        o_ps = ctx.enter_context(nc.psum_tensor("o_ps", [P, HALF], F32))
        sum_ps = ctx.enter_context(nc.psum_tensor("sum_ps", [P, HALF], F32))

        xt_ps = [o_ps, sum_ps]

        def ring(i):
            return st[(i % 4) // 2][:, i % 2, :]

        first_in = sem("first_in")
        tables_in = sem("tables_in")
        rows_made = sem("rows_made")
        half_made = sem("half_made")
        consts_in = sem("consts_in")
        uo_in = sem("uo_in")
        consts_made = sem("consts_made")
        lam_step = sem("lam_step")
        x_in = sem("x_in")
        xr_in = sem("xr_in")
        ln_stat = sem("ln_stat")
        ln_pow = sem("ln_pow")
        ln1_out = sem("ln1_out")
        ln2_out = sem("ln2_out")
        xt_ready = sem("xt_ready")
        xt_out = sem("xt_out")
        ring_ready = sem("ring_ready")
        act_out = sem("act_out")
        wo_added = sem("wo_added")
        swap_in = [sem("swap_q"), sem("swap_k")]
        rope_step = sem("rope_step")
        rope_done = sem("rope_done")
        parts_out = sem("parts_out")
        stack_in = [sem("stack_q"), sem("stack_k")]
        score_ready = sem("score_ready")
        max_done = sem("max_done")
        max_all = sem("max_all")
        max_turned = sem("max_turned")
        shift_step = sem("shift_step")
        shift_made = sem("shift_made")
        shift_in = sem("shift_in")
        st_ready = sem("st_ready")
        exp_done = sem("exp_done")
        pair_added = sem("pair_added")
        av_done = sem("av_done")
        sum_done = sem("sum_done")
        o_read = sem("o_read")
        o_scaled = sem("o_scaled")
        at_ready = sem("at_ready")
        sq_ready = sem("sq_ready")
        rms_inv = sem("rms_inv")
        at_norm = sem("at_norm")
        sum_read = sem("sum_read")
        sum_inv = sem("sum_inv")
        cell_step = sem("cell_step")
        cell_ready = sem("cell_ready")
        x2_out = sem("x2_out")
        z_out = sem("z_out")
        tail_in = [sem(f"tail_in{s}") for s in range(8)]
        tail_add = sem("tail_add")
        tail_tanh = sem("tail_tanh")
        tail_sum = sem("tail_sum")
        tail_out = [sem(f"tail_out{s}") for s in range(8)]

        block = ctx.enter_context(nc.Block())

        def ring_base(b, last):
            return b * PER_ITER + (PRE - (PRE if last else 0))

        def act_base(b, last):
            return b * ACT_ITER + (PRE - (PRE if last else 0))

        def flat(buffer):
            return buffer.rearrange("p a b -> p (a b)")

        tail_x = [flat(q_stack[s // 2][:, 4 * (s % 2):4 * (s % 2) + 4, :].bitcast(F32))
                  for s in range(4)] + [flat(rope_tab[:, 0:2, :]), flat(swapped[:, :, :]),
                                        flat(pair_sum[:, :, :]), flat(xt[:, :, :])]
        tail_z = [flat(k_stack[s // 2][:, 4 * (s % 2):4 * (s % 2) + 4, :].bitcast(F32))
                  for s in range(4)] + [xa[:, :], flat(rope_tab[:, 2:4, :]),
                                        flat(values[:, :, :]), flat(attn_t[:, :, :])]
        SLOTS = len(tail_x)

        N_CONST = 16 * 18

        @block.sync
        def _(sp):
            def value(v):
                return v if isinstance(v, int) else sp.lower_val(v)

            def swap(u, g, ab):
                first = isinstance(u, int) and u == 0
                raw_out = [value(ab + (QK1 if g else QK0) + 2 * X + 2) for X in range(2)]
                before = [value(2 * u - 1 + X) for X in range(2)]
                for X in range(2):
                    sp.wait_ge(act_out, raw_out[X])
                    if not first:
                        sp.wait_ge(rope_done, before[X])
                    for a in range(2):
                        sp.dma_start(swapped[a:P:2, X, :], raw[X][1 - a:P:2, :])\
                          .then_inc(swap_in[X], 16)

            def store_parts(u):
                first = isinstance(u, int) and u == 0
                split = [value(2 * u + X + 1) for X in range(2)]
                stacked = value(16 * BLK * u)
                for X in range(2):
                    sp.wait_ge(rope_done, split[X])
                    if not first:
                        sp.wait_ge(stack_in[X], stacked)
                    sp.dma_start(qk_scr[X, :, :, :].rearrange("a p t -> p a t"), parts[:, :, :])\
                      .then_inc(parts_out, 16)

            def stack(u, g):
                attended = value(64 * (u - 1))
                stored = [value(16 * (2 * u + X + 1)) for X in range(2)]
                if not (isinstance(u, int) and u < 2):
                    sp.wait_ge(st_ready, attended)
                for X in range(2):
                    sp.wait_ge(parts_out, stored[X])
                    for i in range(BLK):
                        dst = (q_stack, k_stack)[X][g]
                        part = (Q_PART, K_PART)[X][i]
                        sp.dma_start(dst[D * i:D * i + D, :, :],
                                     qk_scr[X, part, :, :].rearrange("(j d) t -> d j t", d=D))\
                          .then_inc(stack_in[X], 16)

            def shift_rows(u, g):
                sp.wait_ge(shift_made, u + 1)
                for i in range(3):
                    sp.dma_start(q_stack[g][SROWS + i:SROWS + i + 1, :, :], shift[:, i, :])\
                      .then_inc(shift_in, 16)

            def tail_load(s, b):
                sp.dma_start(tail_z[s], z_scr[b, :, :]).then_inc(tail_in[s], 16)
                sp.dma_start(tail_x[s], x2_scr[b, :, :]).then_inc(tail_in[s], 16)

            def iteration(b, last):
                ab = act_base(b, last)
                u = 2 * b
                if not last:
                    swap(u + 2, 0, ab)
                    store_parts(u + 2)
                shift_rows(u + 1, 1)
                if last:
                    sp.wait_ge(x2_out, 16 * NB)
                    sp.wait_ge(z_out, 16 * NB)
                    sp.wait_ge(ln1_out, TT * (NB + 1))
                    sp.wait_ge(rope_done, 4 * NB)
                    tail_load(4, 4)
                    tail_load(5, 5)
                    sp.wait_ge(st_ready, 64 * (u + 1))
                    tail_load(0, 0)
                    tail_load(1, 1)
                else:
                    stack(u + 2, 0)
                    swap(u + 3, 1, ab)
                    store_parts(u + 3)
                    sp.dma_start(xa[:, :], x[(b + 2) & (NB - 1), :, :]).then_inc(x_in, 16)
                    stack(u + 3, 1)
                sp.wait_ge(sum_done, 32 * b + 31)
                sp.dma_start(x2, x[b, :, :]).then_inc(xr_in, 16)
                if last:
                    sp.wait_ge(st_ready, 64 * (u + 2))
                    tail_load(2, 2)
                    tail_load(3, 3)
                    sp.wait_ge(av_done, 64 * NB)
                    sp.wait_ge(sum_done, 32 * NB)
                    tail_load(6, 6)
                sp.wait_ge(wo_added, 4 * b + 4)
                sp.dma_start(x2_scr[b, :, :], x2).then_inc(x2_out, 16)
                if not last:
                    shift_rows(u + 2, 0)
                sp.wait_ge(act_out, ab + act_index(ZED) + 4)
                sp.dma_start(z_scr[b, :, :], zed).then_inc(z_out, 16)
                if last:
                    tail_load(7, 7)

            sp.dma_start(xa[:, :], x[0, :, :]).then_inc(x_in, 16)
            sp.dma_start(ident[:, :], ident_in).then_inc(first_in, 16)
            for a, w in ((W_Q, wq), (W_K, wk)):
                sp.dma_start(weights[:, a, :, :], w.rearrange("(c p) n -> p c n", p=P))\
                  .then_inc(first_in, 16)
            for a in range(4):
                sp.dma_start(rope_tab[:, a, :], tables[a, :, :]).then_inc(tables_in, 16)
            n = 0
            for a, w in enumerate((wv, wo_attn, wf, wi, wc, uf, ui, uc, wo), W_V):
                sp.dma_start(weights[:, a, :, :], w.rearrange("(c p) n -> p c n", p=P))\
                  .then_inc(consts_in, 16)
                n += 1
            for a in range(4):
                sp.dma_start(lam_in[:, a, :], (lq1, lk1, lq2, lk2)[a]
                             .rearrange("(a n) -> a n", a=1).partition_broadcast(P))\
                  .then_inc(consts_in, 16)
                n += 1
            for a, v in enumerate((bf, bi, bc)):
                sp.dma_start(gate_bias[:, a, :], v)\
                  .then_inc(consts_in, 16)
                n += 1
            sp.dma_start(cell0[:, :], in_c).then_inc(consts_in, 16)
            sp.dma_start(bo_row[:, :], bo.rearrange("(a n) -> a n", a=1)).then_inc(consts_in, 16)
            n += 2
            assert N_CONST == 16 * n
            for u in range(2):
                swap(u, u, 0)
                store_parts(u)
                stack(u, u)
            sp.wait_ge(rope_done, 4)
            sp.dma_start(xa[:, :], x[1, :, :]).then_inc(x_in, 16)
            shift_rows(0, 0)
            with sp.Fori(0, NB - 1) as b:
                iteration(b, False)
            sp.dma_start(weights[:, U_Z, :, :], uo.rearrange("(c p) n -> p c n", p=P))\
              .then_inc(uo_in, 16)
            iteration(NB - 1, True)
            sp.wait_ge(x2_out, 16 * (NB + 1))
            sp.wait_ge(z_out, 16 * (NB + 1))
            with sp.Fori(1, NB // SLOTS) as it:
                for s in range(SLOTS):
                    sp.wait_ge(tail_out[s], 16 * it)
                    tail_load(s, SLOTS * it + s)
            for s in range(SLOTS):
                sp.wait_ge(tail_out[s], 16 * (NB // SLOTS))

        @block.gpsimd
        def _(pool):
            pool.memset(neg_half[:, :], -0.5).then_inc(half_made, 1)
            pool.memset(ones[:, :], 1.0).then_inc(consts_made, 1)
            pool.memset(count_start[:, 0:1], 0.0).then_inc(x2_out, 16)
            pool.memset(count_start[:, 1:2], 0.0).then_inc(z_out, 16)
            pool.memset(rms_eps[:, :], EPS * KEEP ** -2).then_inc(consts_made, 1)

            def pair(u, g, q):
                pool.wait_ge(exp_done, 64 * u + 4 * q + 4)
                if g == 1 or q > 0:
                    pool.wait_ge(sum_done, 16 * u + q)
                a = 2 * q
                pool.tensor_tensor(pair_sum[:, :, :], probs[a % 4][:, :, :],
                                   probs[(a + 1) % 4][:, :, :], ALU.add).then_inc(pair_added, 1)

            def inv_sqrt(n):
                pool.wait_ge(ln_stat, LN_STEPS * (n + 1))
                pool.tensor_tensor(rstd[:, :], var_eps[:, :], neg_half[:, :], ALU.pow)\
                    .then_inc(ln_pow, 1)

            def iteration(b, last):
                for g in range(G):
                    for q in range(4 * ROUNDS):
                        pair(2 * b + g, g, q)
                inv_sqrt(2 * b + 2)
                if not last:
                    inv_sqrt(2 * b + 3)

            pool.wait_ge(half_made, 1)
            inv_sqrt(0)
            inv_sqrt(1)
            with pool.Fori(0, NB - 1) as b:
                iteration(b, False)
            iteration(NB - 1, True)
            with pool.Fori(0, NB // SLOTS) as it:
                for s in range(SLOTS):
                    pool.wait_ge(tail_tanh, SLOTS * it + (s + 1))
                    pool.tensor_tensor(tail_x[s], tail_x[s], tail_z[s], ALU.add)\
                        .then_inc(tail_sum, 1)
                    pool.wait_ge(tail_sum, SLOTS * it + (s + 1))
                    pool.dma_start(out[SLOTS * it + s, :, :], tail_x[s]).then_inc(tail_out[s], 16)

        @block.scalar
        def _(act):
            def take(rb, i, dst, func=ACT.Copy, **kw):
                act.wait_ge(ring_ready, rb + i + 1)
                act.activation(dst, ring(i), func, **kw).then_inc(act_out, 1)

            def take_xt(n):
                for h in range(2):
                    for c in range(KC):
                        act.wait_ge(xt_ready, 4 * n + (2 * h + c + 1))
                        act.activation(xt[:, c, h * HALF:(h + 1) * HALF], xt_ps[c][:, :],
                                       ACT.Copy).then_inc(xt_out, 1)

            def take_qk(rb, u, g):
                for X in range(2):
                    if g == 1:
                        act.wait_ge(rope_done, 2 * u - 1 + X)
                    for h in range(2):
                        take(rb, (QK1 if g else QK0) + 2 * X + h,
                             raw[X][:, h * HALF:(h + 1) * HALF])

            def take_v(rb, places, js):
                for j in js:
                    take(rb, places[j], values[:, 2 * j:2 * j + 2, :].rearrange("p a b -> p (a b)"))

            def copy_o(u, g, r):
                if g == 1 or r > 1:
                    act.wait_ge(at_ready, 2 * u + r // 2)
                act.wait_ge(av_done, 32 * u + 8 * (r + 1))
                act.activation(o_copy[:, r % 2, :], o_ps[:, :], ACT.Copy).then_inc(o_read, 1)

            def copy_sums(u, g, r):
                if g == 1 or r > 0:
                    act.wait_ge(o_scaled, 4 * u + r)
                act.wait_ge(sum_done, 16 * u + 4 * (r + 1))
                act.activation(inv_sum[:, :], sum_ps[:, :], ACT.Copy).then_inc(sum_read, 1)

            def exps(u, g):
                for kk in range(STEPS):
                    if g == 1 or kk >= 4:
                        act.wait_ge(av_done, 32 * u + (kk - 3))
                        act.wait_ge(pair_added, 16 * u + (kk // 2 - 1))
                    for hp in range(2):
                        act.wait_ge(st_ready, 64 * u + (2 * kk + hp + 1))
                        act.activation(probs[kk % 4][:, 2 * hp:2 * hp + 2, :], st[hp][:, :, :],
                                       ACT.Exp).then_inc(exp_done, 1)
                    if kk % 8 == 0 and kk:
                        copy_o(u, g, kk // 8 - 1)
                    if kk % 8 == 3 and kk > 8:
                        copy_sums(u, g, kk // 8 - 1)
                copy_o(u, g, 3)

            def iteration(b, last):
                rb, ab = ring_base(b, last), act_base(b, last)
                if not last:
                    take_xt(2 * b + 1)
                    take_qk(rb, 2 * b + 2, 0)
                act.wait_ge(x2_out, 16 * b + 16)
                act.wait_ge(z_out, 16 * b + 16)
                act.wait_ge(cell_ready, 4 * b + 1)
                exps(2 * b, 0)
                if not last:
                    take_qk(rb, 2 * b + 3, 1)
                copy_sums(2 * b, 0, 3)
                exps(2 * b + 1, 1)
                if not last:
                    take_v(rb, VAL, (0, 1))
                copy_sums(2 * b + 1, 1, 3)
                squares_at = LAST_RMS if last else RMS
                for quarters in ((0, 1, 2), (3,)):
                    for i in quarters:
                        take(rb, squares_at[i], rms[:, i, :], ACT.Ln, scale=KEEP ** -2 / (2 * D),
                             bias=rms_eps[:, 0:1])
                    for i in quarters:
                        act.wait_ge(act_out, ab + (squares_at[i] + 1))
                        act.activation(rms[:, i, :], rms[:, i, :], ACT.Exp, scale=-0.5)\
                           .then_inc(rms_inv, 1)
                    if not last and i == 2:
                        take_v(rb, VAL, (2, 3))
                take_xt(2 * b + (1 if last else 2))
                for h in range(2):
                    for m in range(KC):
                        if h == 1:
                            act.wait_ge(cell_ready, 4 * b + (2 + m))
                        for a, func in enumerate((ACT.Sigmoid, ACT.Sigmoid, ACT.Tanh)):
                            take(rb, GATE + 6 * h + 3 * m + a, gates[m][:, a, :], func,
                                 bias=gate_bias[:, a, m:m + 1])
                for j in range(4):
                    take(rb, ZED + j, zed[:, 2 * j * E:2 * (j + 1) * E])

            take_xt(0)
            take_qk(0, 0, 0)
            act.wait_ge(lam_step, 4)
            act.activation(lam_exp[:, :], lam_dot[:, :], ACT.Exp).then_inc(lam_step, 1)
            act.wait_ge(consts_in, N_CONST)
            act.wait_ge(consts_made, 4)
            take_qk(0, 1, 1)
            take_v(0, range(VAL[0], PRE), range(4))
            with act.Fori(0, NB - 1) as b:
                iteration(b, False)
            iteration(NB - 1, True)
            rb = ring_base(NB - 1, True)
            act.wait_ge(x2_out, 16 * (NB + 1))
            for j in range(4):
                take(rb, GEE + j, x2[:, 2 * j * E:2 * (j + 1) * E])
            with act.Fori(0, NB // SLOTS) as it:
                for s in range(SLOTS):
                    act.wait_ge(tail_add, SLOTS * it + (s + 1))
                    act.activation(tail_z[s], tail_z[s], ACT.Tanh).then_inc(tail_tanh, 1)

        @block.tensor
        def _(pe):
            def turn(i, b, ab):
                p = i - 4
                if WO <= p < WO + 4:
                    pe.wait_ge(wo_added, 4 * b + (p - WO + 1))
                elif not (isinstance(ab, int) and ab + p + 1 <= 0):
                    pe.wait_ge(act_out, ab + (act_index(p) + 1))

            def transposes(src, ln_out, m, n):
                for h in range(2):
                    pe.wait_ge(ln_out, TT * m + (4 * h + 4))
                    for c in range(KC):
                        if h == 1:
                            pe.wait_ge(xt_out, 4 * n + (c + 1))
                        for t in range(4):
                            at = (4 * h + t) * E + c * P
                            mm = pe.transpose(xt_ps[c][:, t * P:(t + 1) * P], src[:, at:at + P],
                                              ident[:, :])
                        mm.then_inc(xt_ready, 1)

            def qk(g, b, ab, blocks=iter(())):
                for X in range(2):
                    for h in range(2):
                        i = (QK1 if g else QK0) + 2 * X + h
                        turn(i, b, ab)
                        for c in range(KC):
                            mm = pe.matmul(ring(i), weights[:, W_Q + X, c, g * P:(g + 1) * P],
                                           xt[:, c, h * HALF:(h + 1) * HALF],
                                           start=(c == 0), stop=(c == KC - 1))
                            for n in itertools.islice(blocks, 1):
                                score(2 * b + 1, 1, n)
                        mm.then_inc(ring_ready, 1)

            def rows_out(first, w, src, b, ab, bias=False, js=range(4), beside=(0, 0, iter(()))):
                un, un_group, blocks = beside
                for j in js:
                    i = first[j] if isinstance(first, tuple) else first + j
                    turn(i, b, ab)
                    for t in range(2):
                        dst = ring(i)[:, t * E:(t + 1) * E]
                        at = (2 * j + t) * P
                        for c in range(KC):
                            mm = pe.matmul(dst, src[:, c, at:at + P], weights[:, w, c, :],
                                           start=(c == 0), stop=(c == KC - 1 and not bias))
                            for n in itertools.islice(blocks, 1):
                                score(un, un_group, n)
                        if bias:
                            mm = pe.matmul(dst, ones[0:1, :], bo_row[:, :], start=False,
                                           stop=True)
                    mm.then_inc(ring_ready, 1)

            def score(u, g, i):
                s, t, h = i // 16, i % 16 // 2, i % 2
                if i >= 2:
                    pe.wait_ge(max_done, SCORES * u + (i - 1))
                pe.matmul(s_ps[i % 2][:, :], q_stack[g][0:SROWS, s, t * P:(t + 1) * P],
                          k_stack[g][0:SROWS, s, h * HALF:(h + 1) * HALF],
                          start=True, stop=True).then_inc(score_ready, 1)

            def score_start(u):
                pe.wait_ge(stack_in[0], 16 * BLK * (u + 1))
                pe.wait_ge(stack_in[1], 16 * BLK * (u + 1))
                if not (isinstance(u, int) and u == 0):
                    pe.wait_ge(shift_made, u)

            def turn_max(u):
                pe.wait_ge(max_all, u + 1)
                pe.transpose(s_ps[0][:, 0:P], neg_max[:, :], ident[:, :])\
                    .then_inc(max_turned, 1)

            def key_tile(u, g, kk, hp):
                th, sub, kt = kk // 16, kk // 8 % 2, kk % 8
                if kk >= 1:
                    pe.wait_ge(exp_done, 64 * u + (2 * kk + hp - 1))
                for j in range(2):
                    s = 2 * (2 * hp + j) + sub
                    mm = pe.matmul(st[hp][:, j, :],
                                   k_stack[g][0:KROWS, s, kt * P:(kt + 1) * P],
                                   q_stack[g][0:KROWS, s, th * HALF:(th + 1) * HALF],
                                   start=True, stop=True)
                mm.then_inc(st_ready, 1)

            def weighted(u, g, kk):
                r, kt = kk // 8, kk % 8
                pe.wait_ge(exp_done, 64 * u + (2 * kk + 2))
                if kt == 0 and (g == 1 or r > 0):
                    pe.wait_ge(o_read, 4 * u + r)
                for h in range(4):
                    at = (4 * g + h) * 2 * D
                    mm = pe.matmul(o_ps[32 * h:32 * h + 32, :], values[:, kt, at:at + 2 * D],
                                   probs[kk % 4][:, h, :], start=(kt == 0), stop=(kt == KT - 1))
                mm.then_inc(av_done, 1)

            def key_sums(u, g, q):
                r, p = q // 4, q % 4
                pe.wait_ge(pair_added, 16 * u + (q + 1))
                if p == 0 and (g == 1 or r > 0):
                    pe.wait_ge(sum_read, 4 * u + r)
                for h in range(4):
                    mm = pe.matmul(sum_ps[32 * h:32 * h + 32, :], ones[:, 0:32],
                                   pair_sum[:, h, :], start=(p == 0), stop=(p == 3))
                mm.then_inc(sum_done, 1)

            def attention(u, g, un, plan):
                pe.wait_ge(shift_in, 48 * (u + 1))
                for s in range(STEPS):
                    todo = list(plan[s])
                    key_tile(u, g, s, 0)
                    if todo and todo[0] == 0:
                        score_start(un)
                    for i in todo[0:1]:
                        score(un, 1 - g, i)
                    key_tile(u, g, s, 1)
                    for i in todo[1:2]:
                        score(un, 1 - g, i)
                    if s >= 1:
                        weighted(u, g, s - 1)
                    for i in todo[2:4]:
                        score(un, 1 - g, i)
                    if s >= 4 and s % 2 == 0:
                        key_sums(u, g, (s - 4) // 2)
                    for i in todo[4:]:
                        score(un, 1 - g, i)
                weighted(u, g, STEPS - 1)
                key_sums(u, g, 14)

            def iteration(b, last):
                ab = act_base(b, last)
                u = 2 * b
                if not last:
                    transposes(xa, ln1_out, b + 1, 2 * b + 1)
                    pe.wait_ge(xt_out, 4 * (2 * b + 2))
                    qk(0, b, ab, iter(range(BEFORE, sum(EARLY))))
                    pe.wait_ge(act_out, ab + QK0 + 4)
                else:
                    for i in range(BEFORE, sum(EARLY)):
                        score(u + 1, 1, i)
                    pe.wait_ge(act_out, ab + PRE)
                attention(u, 0, u + 1, PLAN0)
                turn_max(u + 1)
                if not last:
                    qk(1, b, ab)
                key_sums(u, 0, 15)
                if not last:
                    pe.wait_ge(act_out, ab + QK1 + 4)
                attention(u + 1, 1, u + 2, NO_PLAN if last else PLAN1)
                late = iter(range(SCORES - sum(LATE), SCORES))
                if not last:
                    rows_out(VAL, W_V, xt, b, ab, js=(0, 1),
                             beside=(u + 2, 0, itertools.islice(late, LATE[0])))
                key_sums(u + 1, 1, 15)

                squares_at = LAST_RMS if last else RMS

                def mean_square(i):
                    pe.wait_ge(sq_ready, 4 * b + (i + 1))
                    turn(squares_at[i], b, ab)
                    pe.matmul(ring(squares_at[i]), head_ones[:, :], square[:, i, :], start=True,
                              stop=True).then_inc(ring_ready, 1)

                for i in range(3):
                    mean_square(i)
                if not last:
                    rows_out(VAL, W_V, xt, b, ab, js=(2, 3))
                mean_square(3)
                beside = (u + 2, 0, iter(()) if last else itertools.islice(late, sum(LATE[1:4])))
                pe.wait_ge(at_norm, 4 * b + 2)
                rows_out(WO, W_O, attn_t, b, ab, js=(0, 1), beside=beside)
                pe.wait_ge(at_norm, 4 * b + 4)
                rows_out(WO, W_O, attn_t, b, ab, js=(2, 3), beside=beside)
                early = iter(range(BEFORE))

                def gate_part(i, cell, start, stop):
                    h, m, a = i // 6, i % 6 // 3, i % 3
                    hs, ms = slice(h * HALF, (h + 1) * HALF), slice(m * P, (m + 1) * P)
                    for c in range(KC):
                        mm = pe.matmul(ring(GATE + i),
                                       weights[:, (U_F if cell else W_F) + a, c, ms],
                                       (cell_t if cell else xt)[:, c, hs],
                                       start=(start and c == 0), stop=(stop and c == KC - 1))
                        if not last and i in (4, 5, 6):
                            for n in itertools.islice(late, 1):
                                score(u + 2, 0, n)
                        if not last and i >= 8:
                            for n in itertools.islice(early, 1):
                                if n == 0:
                                    score_start(u + 3)
                                score(u + 3, 1, n)
                    return mm

                pe.wait_ge(cell_ready, 4 * b + 1)
                for i in range(4):
                    turn(GATE + i, b, ab)
                    gate_part(i, True, True, False)
                transposes(xn2, ln2_out, b, 2 * b + (1 if last else 2))
                pe.wait_ge(xt_out, 4 * (2 * b + (2 if last else 3)))
                for i in range(4):
                    gate_part(i, False, False, True).then_inc(ring_ready, 1)
                for i in range(4, 12):
                    if i == 7 and not last:
                        turn_max(u + 2)
                    turn(GATE + i, b, ab)
                    gate_part(i, True, True, False)
                    gate_part(i, False, False, True).then_inc(ring_ready, 1)
                rows_out(ZED, W_Z, xt, b, ab, js=(0,))
                rows_out(ZED, W_Z, xt, b, ab, js=(1, 2, 3),
                         beside=(u + 3, 1, iter(()) if last else early))
                assert last or not list(early)

            pe.wait_ge(first_in, 48)
            transposes(xa, ln1_out, 0, 0)
            pe.wait_ge(xt_out, 4)
            qk(0, 0, 0)
            qk(1, 0, 0)
            pe.wait_ge(consts_in, N_CONST)
            pe.wait_ge(consts_made, 4)
            rows_out(VAL[0], W_V, xt, 0, 0)
            score_start(0)
            for i in range(SCORES):
                score(0, 0, i)
            turn_max(0)
            score_start(1)
            for i in range(BEFORE):
                score(1, 1, i)
            pe.wait_ge(rows_made, 2)
            with pe.Fori(0, NB - 1) as b:
                iteration(b, False)
            iteration(NB - 1, True)
            pe.wait_ge(cell_ready, 4 * NB + 1)
            pe.wait_ge(uo_in, 16)
            rows_out(GEE, U_Z, cell_t, NB - 1, act_base(NB - 1, True), bias=True)

        @block.vector
        def _(dve):
            def norm_stats(n, src):
                for t in range(TT):
                    dve.bn_stats(stats[:, t, :], src[:, t * E:(t + 1) * E]).then_inc(ln_stat, 1)
                even, odd = stats[:, :, 0:3], stats[:, :, 3:6]
                dve.wait_ge(ln_stat, LN_STEPS * n + TT)
                dve.tensor_tensor(ln_sum[:, :], even[:, :, 1], odd[:, :, 1], ALU.add)\
                   .then_inc(ln_stat, 1)
                dve.tensor_tensor(ln_diff[:, :], even[:, :, 1], odd[:, :, 1], ALU.subtract)\
                   .then_inc(ln_stat, 1)
                dve.tensor_tensor(ln_square[:, :], even[:, :, 2], odd[:, :, 2], ALU.add)\
                   .then_inc(ln_stat, 1)
                dve.wait_ge(ln_stat, LN_STEPS * n + TT + 3)
                dve.tensor_scalar(mean[:, :], ln_sum[:, :], 0.5, None, ALU.mult)\
                   .then_inc(ln_stat, 1)
                dve.scalar_tensor_tensor(out=ln_between[:, :], in0=ln_diff[:, :], scalar=0.25,
                                         in1=ln_diff[:, :], op0=ALU.mult, op1=ALU.mult)\
                   .then_inc(ln_stat, 1)
                dve.tensor_scalar(ln_square[:, :], ln_square[:, :], 1.0 / E, EPS, ALU.mult,
                                  ALU.add).then_inc(ln_stat, 1)
                dve.wait_ge(ln_stat, LN_STEPS * n + TT + 6)
                dve.tensor_tensor(var_eps[:, :], ln_square[:, :], ln_between[:, :], ALU.add)\
                   .then_inc(ln_stat, 1)

            def normalise(n, src, dst, ln_out):
                dve.wait_ge(ln_pow, n + 1)
                for t in range(TT):
                    dve.tensor_scalar(dst[:, t * E:(t + 1) * E], src[:, t * E:(t + 1) * E],
                                      mean[:, t:t + 1], rstd[:, t:t + 1], ALU.subtract,
                                      ALU.mult).then_inc(ln_out, 1)

            def rope(u, steps=range(14)):
                for X, k in (divmod(step, 7) for step in steps):
                    n = 2 * u + X
                    if k == 0:
                        dve.wait_ge(swap_in[X], 32 * (u + 1))
                        dve.tensor_tensor(raw[X], raw[X], rope_tab[:, 2 * X, :], ALU.mult)\
                           .then_inc(rope_step, 1)
                    if k == 1:
                        dve.tensor_tensor(swapped[:, X, :], swapped[:, X, :],
                                          rope_tab[:, 2 * X + 1, :], ALU.mult)\
                           .then_inc(rope_step, 1)
                    if k == 2:
                        dve.wait_ge(rope_step, 6 * n + 2)
                        dve.tensor_tensor(raw[X], raw[X], swapped[:, X, :], ALU.add)\
                           .then_inc(rope_step, 1)
                    if k == 3:
                        dve.wait_ge(rope_step, 6 * n + 3)
                        if not (isinstance(n, int) and n == 0):
                            dve.wait_ge(parts_out, 16 * n)
                        dve.tensor_copy(parts[:, 0, :], raw[X]).then_inc(rope_step, 1)
                    if k == 4:
                        dve.wait_ge(rope_step, 6 * n + 4)
                        dve.tensor_tensor(swapped[:, X, :], raw[X], parts[:, 0, :],
                                          ALU.subtract).then_inc(rope_step, 1)
                    if k == 5:
                        dve.wait_ge(rope_step, 6 * n + 5)
                        dve.tensor_copy(parts[:, 1, :], swapped[:, X, :]).then_inc(rope_step, 1)
                    if k == 6:
                        dve.wait_ge(rope_step, 6 * n + 6)
                        dve.tensor_tensor(parts[:, 2, :], swapped[:, X, :], parts[:, 1, :],
                                          ALU.subtract).then_inc(rope_done, 1)

            def maximum(u, i):
                dve.wait_ge(score_ready, SCORES * u + (i + 1))
                dve.tensor_reduce(neg_max2[:, i // 2, i % 2:i % 2 + 1], s_ps[i % 2][:, :], AX.X,
                                  ALU.max, negate=True).then_inc(max_done, 1)

            def join_max(u):
                dve.wait_ge(max_done, SCORES * (u + 1))
                dve.tensor_reduce(neg_max[:, 0:SUBS * TT], neg_max2[:, :, :], AX.X, ALU.min)\
                   .then_inc(max_all, 1)

            def split_shift(u):
                src = s_ps[0][0:SUBS * TT, 0:P]
                dve.wait_ge(max_turned, u + 1)
                if not (isinstance(u, int) and u == 0):
                    dve.wait_ge(shift_in, 48 * u)
                dve.tensor_copy(shift[:, 0, :], src).then_inc(shift_step, 1)
                dve.wait_ge(shift_step, 3 * u + 1)
                dve.tensor_tensor(shift_rest[:, :], src, shift[:, 0, :], ALU.subtract)\
                   .then_inc(shift_step, 1)
                dve.wait_ge(shift_step, 3 * u + 2)
                dve.tensor_copy(shift[:, 1, :], shift_rest[:, :]).then_inc(shift_step, 1)
                dve.wait_ge(shift_step, 3 * u + 3)
                dve.tensor_tensor(shift[:, 2, :], shift_rest[:, :], shift[:, 1, :],
                                  ALU.subtract).then_inc(shift_made, 1)

            def invert_sums(u, r, part):
                if part == 0:
                    dve.wait_ge(sum_read, 4 * u + (r + 1))
                cols = inv_sum[:, part * P:(part + 1) * P]
                dve.reciprocal(cols, cols).then_inc(sum_inv, 1)

            def divide(u, g, r):
                dve.wait_ge(sum_inv, 16 * u + 4 * (r + 1))
                dve.wait_ge(o_read, 4 * u + (r + 1))
                dve.tensor_tensor(o_copy[:, r % 2, :], o_copy[:, r % 2, :], inv_sum[:, :],
                                  ALU.mult).then_inc(o_scaled, 1)
                if r % 2 == 1:
                    th = r // 2
                    dve.wait_ge(o_scaled, 4 * u + (r + 1))
                    dve.scalar_tensor_tensor(out=attn_t[:, g, th * HALF:(th + 1) * HALF],
                                             in0=o_copy[:, 1, :], scalar=neg_lam[:, 0:1],
                                             in1=o_copy[:, 0, :], op0=ALU.mult, op1=ALU.add)\
                       .then_inc(at_ready, 1)

            def attention(u, g, un, plan, turned=None):
                for s in range(STEPS):
                    for i in plan[s]:
                        maximum(un, i)
                    if turned is not None and s in ROPE_AT:
                        rope(turned, [ROPE_AT.index(s)])
                    if s > 8 and 3 <= s % 8 <= 6:
                        invert_sums(u, s // 8 - 1, s % 8 - 3)
                    if s > 8 and s % 8 == 7:
                        divide(u, g, s // 8 - 1)

            def iteration(b, last):
                rb, ab = ring_base(b, last), act_base(b, last)
                u = 2 * b
                for i in range(BEFORE, sum(EARLY)):
                    maximum(u + 1, i)
                attention(u, 0, u + 1, PLAN0, None if last else u + 2)
                join_max(u + 1)
                split_shift(u + 1)
                for k in range(4):
                    invert_sums(u, 3, k)
                divide(u, 0, 3)
                attention(u + 1, 1, u + 2, NO_PLAN if last else PLAN1,
                          None if last else u + 3)
                late, early = iter(range(SCORES - sum(LATE), SCORES)), iter(range(BEFORE))

                def part(i):
                    th, g = divmod(i, 2)
                    return attn_t[:, g, th * HALF:(th + 1) * HALF]

                def squares(i):
                    dve.tensor_tensor(square[:, i, :], part(i), part(i), ALU.mult)\
                       .then_inc(sq_ready, 1)

                def at_times_rms(i):
                    dve.wait_ge(rms_inv, 4 * b + (i + 1))
                    dve.tensor_tensor(part(i), part(i), rms[:, i, :], ALU.mult)\
                       .then_inc(at_norm, 1)

                def maxima(un, blocks, n):
                    if not last:
                        for i in itertools.islice(blocks, n):
                            maximum(un, i)

                dve.wait_ge(at_ready, 4 * b + 3)
                dve.wait_ge(sum_done, 32 * b + 31)
                for i in range(3):
                    squares(i)
                maxima(u + 2, late, LATE[0])
                for k in range(4):
                    invert_sums(u + 1, 3, k)
                divide(u + 1, 1, 3)
                dve.wait_ge(at_ready, 4 * b + 4)
                squares(3)
                for i in range(3):
                    at_times_rms(i)
                maxima(u + 2, late, LATE[1])
                at_times_rms(3)
                maxima(u + 2, late, LATE[2])
                dve.wait_ge(xr_in, 16 * (b + 1))
                for j in range(4):
                    rows = x2[:, 2 * j * E:2 * (j + 1) * E]
                    dve.wait_ge(ring_ready, rb + (WO + j + 1))
                    dve.tensor_tensor(rows, ring(WO + j), rows, ALU.add).then_inc(wo_added, 1)
                    if j == 1:
                        maxima(u + 2, late, LATE[3])
                dve.wait_ge(wo_added, 4 * b + 4)
                norm_stats(u + 2, x2)
                normalise(u + 2, x2, xn2, ln2_out)
                if not last:
                    dve.wait_ge(x_in, 16 * b + 48)
                    norm_stats(u + 3, xa)
                    normalise(u + 3, xa, xa, ln1_out)
                    maxima(u + 2, late, LATE[4])
                    join_max(u + 2)
                cells(b, ab, 0)
                if not last:
                    split_shift(u + 2)
                maxima(u + 3, early, EARLY[0])
                cells(b, ab, 1)
                maxima(u + 3, early, EARLY[1])

            def cells(b, ab, h):
                dve.wait_ge(act_out, ab + (act_index(GATE) + 6 * h + 6))
                for m in range(KC):
                    f, i, a = (gates[m][:, j, :] for j in range(3))
                    c = cell_t[:, m, h * HALF:(h + 1) * HALF]
                    dve.tensor_tensor(i, i, a, ALU.mult).then_inc(cell_step, 1)
                    dve.tensor_tensor(f, f, c, ALU.mult).then_inc(cell_step, 1)
                    dve.wait_ge(cell_step, 8 * b + (4 * h + 2 * m + 2))
                    dve.tensor_tensor(c, f, i, ALU.add).then_inc(cell_ready, 1)

            dve.wait_ge(x_in, 16)
            norm_stats(0, xa)
            normalise(0, xa, xa, ln1_out)
            dve.memset(head_ones[:, :], 0.0).then_inc(lam_step, 1)
            dve.wait_ge(lam_step, 1)
            for h in range(4):
                mm = dve.memset(head_ones[32 * h:32 * h + 32, 32 * h:32 * h + 32], 1.0)
            mm.then_inc(consts_made, 1)
            dve.wait_ge(consts_in, N_CONST)
            for a in range(2):
                dve.tensor_tensor(lam_prod[:, a, :], lam_in[:, 2 * a, :], lam_in[:, 2 * a + 1, :],
                                  ALU.mult).then_inc(lam_step, 1)
            dve.wait_ge(lam_step, 3)
            dve.tensor_reduce(lam_dot[:, :], lam_prod[:, :, :], AX.X, ALU.add)\
               .then_inc(lam_step, 1)
            dve.memset(neg_max[:, SUBS * TT:P], 0.0)
            dve.memset(cell_t[:, :, :], 0.0).then_inc(consts_made, 1)
            dve.wait_ge(consts_made, 4)
            for c in range(KC):
                mm = dve.tensor_scalar(cell_t[:, c, :], cell_t[:, c, :], cell0[:, c:c + 1], None,
                                       ALU.add)
            mm.then_inc(cell_ready, 1)
            dve.wait_ge(tables_in, 64)
            rope(0)
            for g in range(G):
                dve.memset(k_stack[g][SROWS:P, :, :], 1.0).then_inc(rows_made, 1)
            dve.wait_ge(lam_step, 5)
            dve.tensor_tensor(neg_lam[:, :], lam_exp[:, 1:2], lam_exp[:, 0:1], ALU.subtract)\
               .then_inc(lam_step, 1)
            dve.wait_ge(lam_step, 6)
            dve.tensor_scalar(neg_lam[:, :], neg_lam[:, :], -LAMBDA_INIT, None, ALU.add)\
               .then_inc(lam_step, 1)
            rope(1)
            for i in range(SCORES):
                maximum(0, i)
            join_max(0)
            split_shift(0)
            dve.wait_ge(x_in, 32)
            norm_stats(1, xa)
            normalise(1, xa, xa, ln1_out)
            for i in range(BEFORE):
                maximum(1, i)
            dve.wait_ge(lam_step, 7)
            with dve.Fori(0, NB - 1) as b:
                iteration(b, False)
            iteration(NB - 1, True)
            dve.wait_ge(act_out, act_base(NB - 1, True) + act_index(GEE) + 4)
            with dve.Fori(0, NB // SLOTS) as it:
                for s in range(SLOTS):
                    dve.wait_ge(tail_in[s], 32 * it + 32)
                    dve.tensor_tensor(tail_z[s], tail_z[s], x2, ALU.add).then_inc(tail_add, 1)


def rope_tables():
    f32 = np.float32
    even = np.arange(0, D, 2, dtype=f32)
    inv_freq = f32(1.0) / np.power(f32(10000.0), even / f32(D), dtype=f32)
    pos = np.arange(T, dtype=f32)
    freqs = np.repeat(pos[:, None] * inv_freq[None, :], 2, axis=-1).astype(np.float64)
    sv = (even + f32(0.4 * D)) / f32(1.4 * D)
    power = (pos - T // 2) / f32(512.0)
    scale = np.power(sv[None, :].astype(np.float64), power[:, None].astype(np.float64))
    scale = np.concatenate([scale, scale], axis=-1)
    cos, sin = np.cos(freqs), np.sin(freqs)
    sin[:, 0::2] *= -1.0
    q, k = scale * D ** -0.5, 1.0 / scale
    token = (np.arange(P)[None, :] * TT + np.arange(TT)[:, None]).reshape(-1)
    tabs = [np.tile(a[token].T, (SUBS, 1)) for a in (cos * q, sin * q, cos * k, sin * k)]
    return np.ascontiguousarray(np.stack(tabs).astype(f32))


_NAMES = ["attn_Wq", "attn_Wk", "attn_Wv", "attn_Wo", "attn_lambda_q1", "attn_lambda_k1",
          "attn_lambda_q2", "attn_lambda_k2", "ffn_wf", "ffn_uf", "ffn_bf", "ffn_wi", "ffn_ui",
          "ffn_bi", "ffn_wc", "ffn_uc", "ffn_bc", "ffn_wo", "ffn_uo", "ffn_bo", "ffn_in_c"]


def kernel(**inputs):
    import concourse.bacc as _bacc
    from concourse.bass_utils import run_bass_kernel_spmd as _run

    nc = _bacc.Bacc("TRN2", target_bir_lowering=False, num_devices=1)
    arrays = {"x": np.ascontiguousarray(inputs["L0_attn_x"]).reshape(NB, P, TT * E)}
    for name in _NAMES:
        a = np.asarray(inputs["L0_" + name])
        if name in ("ffn_bf", "ffn_bi", "ffn_bc", "ffn_in_c"):
            a = a.reshape(KC, P)
        arrays[name] = np.ascontiguousarray(a.T)
    arrays["rope_tables"] = rope_tables()
    arrays["identity"] = np.eye(P, dtype=np.float32)
    args = [nc.dram_tensor("in_" + n, a.shape, mybir.dt.from_np(a.dtype),
                           kind="ExternalInput").ap() for n, a in arrays.items()]
    out = nc.dram_tensor("out_rows", (NB, P, TT * E), F32, kind="ExternalOutput").ap()
    build(nc, *args, out)
    r = _run(nc, [{"in_" + n: a for n, a in arrays.items()}], core_ids=[0])
    return r.results[0]["out_rows"].reshape(NB, T, E)
```
